# Optimizing a Trainium2 kernel written in Bass

```python
import numpy as np
import jax
import jax.numpy as jnp

def _softmax(x, axis=-1):
    return jax.nn.softmax(x, axis=axis)

def _gelu(x):
    return jax.nn.gelu(x, approximate=True)

def _silu(x):
    return jax.nn.silu(x)

def _sigmoid(x):
    return jax.nn.sigmoid(x)

def _layernorm(x, axis=-1, eps=1e-05):
    m = jnp.mean(x, axis=axis, keepdims=True)
    v = jnp.var(x, axis=axis, keepdims=True)
    return (x - m) / jnp.sqrt(v + eps)

def _scatter_add(tgt, idx, src, axis=0):
    return tgt.at[idx].add(src)

def _segment_sum(src, seg, n):
    return jax.ops.segment_sum(src, seg, n)
kernel_name = 'mk_lm_tower_d1_tok_ids512_r4_286baa'

def setup_inputs(seed: int=0):
    np.random.seed(seed)
    _w = jnp.asarray

    def _rec_inputs():
        import jax
        import jax.numpy as jnp
        _rk = jax.random.key(seed)
        x = jax.random.randint(jax.random.fold_in(_rk, 1), (16, 1024), 0, 3750, jnp.int32)
        return x
    x = _rec_inputs()

    def _L0_tok_setup():
        import jax, jax.numpy as jnp
        import numpy as np
        VOCAB = 3750
        EMB = 128
        HID = 128
        N_LAYERS = 6
        KSIZE = 3
        SCALE = 0.7071067811865476

        def _conv1d_same(x, w, b):
            y = jax.lax.conv_general_dilated(x, w, window_strides=(1,), padding='SAME', dimension_numbers=('NCH', 'OIH', 'NCH'))
            return y + b[None, :, None]
        key = jax.random.key(seed)
        ks = jax.random.split(key, 8)
        src = jax.random.randint(ks[0], (32, 512), 0, VOCAB)
        emb_table = jax.random.normal(ks[1], (VOCAB, EMB), dtype=jnp.float32) * 0.02
        W_e2h = jax.random.normal(ks[2], (EMB, HID), dtype=jnp.float32) * 0.02
        b_e2h = jnp.zeros((HID,), dtype=jnp.float32)
        conv_w = jax.random.normal(ks[3], (N_LAYERS, 2 * HID, HID, KSIZE), dtype=jnp.float32) * 0.02
        conv_b = jnp.zeros((N_LAYERS, 2 * HID), dtype=jnp.float32)
        W_h2e = jax.random.normal(ks[4], (HID, EMB), dtype=jnp.float32) * 0.02
        b_h2e = jnp.zeros((EMB,), dtype=jnp.float32)
        return {'src': src, 'emb_table': emb_table, 'W_e2h': W_e2h, 'b_e2h': b_e2h, 'conv_w': conv_w, 'conv_b': conv_b, 'W_h2e': W_h2e, 'b_h2e': b_h2e}
    _L0_tok_all = _L0_tok_setup()
    _L0_tok_in = {k: v for k, v in _L0_tok_all.items() if k in ('emb_table', 'W_e2h', 'b_e2h', 'conv_w', 'conv_b', 'W_h2e', 'b_h2e')}
    del _L0_tok_all

    def _L0_attn_setup():
        import jax, jax.numpy as jnp
        import numpy as np
        B, L, D, H = (4, 256, 128, 8)
        HD = D // H

        def _window_size(L):
            for cand in (5, 4, 3, 2):
                if L % cand == 0:
                    return cand
            return 5

        def _window_stats(attn, ws):
            b, h, l, _ = attn.shape
            nw = l // ws
            r = attn.reshape(b, h, nw, ws, l)
            mean = r.mean(axis=(-1, -2))
            std = jnp.std(r, axis=-1, ddof=1).mean(axis=-1)
            mx = r.max(axis=-1).mean(axis=-1)
            mn = r.min(axis=-1).mean(axis=-1)
            return jnp.stack([mean, std, mx, mn], axis=-1)
        key = jax.random.key(seed)
        ks = jax.random.split(key, 13)
        s = 0.02
        return {'x': jax.random.normal(ks[0], (B, L, D), jnp.float32), 'Wq1': jax.random.normal(ks[1], (D, D), jnp.float32) * s, 'Wk1': jax.random.normal(ks[2], (D, D), jnp.float32) * s, 'Wq2': jax.random.normal(ks[3], (D, D), jnp.float32) * s, 'Wk2': jax.random.normal(ks[4], (D, D), jnp.float32) * s, 'Wv': jax.random.normal(ks[5], (D, D), jnp.float32) * s, 'Wo': jax.random.normal(ks[6], (D, D), jnp.float32) * s, 'gw1': jax.random.normal(ks[7], (8, 32), jnp.float32) * 0.1, 'gb1': jnp.zeros((32,), jnp.float32), 'gw2': jax.random.normal(ks[8], (32, 16), jnp.float32) * 0.1, 'gb2': jnp.zeros((16,), jnp.float32), 'gw3': jax.random.normal(ks[9], (16, 1), jnp.float32) * 0.1, 'gb3': jnp.zeros((1,), jnp.float32)}
    _L0_attn_all = _L0_attn_setup()
    _L0_attn_in = {k: v for k, v in _L0_attn_all.items() if k in ('Wq1', 'Wk1', 'Wq2', 'Wk2', 'Wv', 'Wo', 'gw1', 'gb1', 'gw2', 'gb2', 'gw3', 'gb3')}
    del _L0_attn_all

    def _L0_ffn_setup():
        import jax, jax.numpy as jnp
        import numpy as np
        MICRO_BATCHES = 2
        TOP_K = 2
        D = 128
        E = 8
        B, S = (8, 2048)
        key = jax.random.key(seed)
        ks = jax.random.split(key, 12)
        s = 0.02
        return {'x': jax.random.normal(ks[0], (B, S, D), dtype=jnp.float32), 'ln_g': jnp.ones((D,), jnp.float32), 'ln_b': jnp.zeros((D,), jnp.float32), 'attn_w': jax.random.normal(ks[1], (D, D), jnp.float32) * s, 'attn_b': jnp.zeros((D,), jnp.float32), 'gate_w': jax.random.normal(ks[2], (E, D), jnp.float32) * s, 'fc1_w': jax.random.normal(ks[3], (E, 4 * D, D), jnp.float32) * s, 'fc1_b': jnp.zeros((E, 4 * D), jnp.float32), 'fc2_w': jax.random.normal(ks[4], (E, D, 4 * D), jnp.float32) * s, 'fc2_b': jnp.zeros((E, D), jnp.float32), 'next_w': jax.random.normal(ks[5], (D, D), jnp.float32) * s, 'next_b': jnp.zeros((D,), jnp.float32)}
    _L0_ffn_all = _L0_ffn_setup()
    _L0_ffn_in = {k: v for k, v in _L0_ffn_all.items() if k in ('ln_g', 'ln_b', 'attn_w', 'attn_b', 'gate_w', 'fc1_w', 'fc1_b', 'fc2_w', 'fc2_b', 'next_w', 'next_b')}
    del _L0_ffn_all
    return {'x': x, 'L0_tok_emb_table': _L0_tok_in['emb_table'], 'L0_tok_W_e2h': _L0_tok_in['W_e2h'], 'L0_tok_b_e2h': _L0_tok_in['b_e2h'], 'L0_tok_conv_w': _L0_tok_in['conv_w'], 'L0_tok_conv_b': _L0_tok_in['conv_b'], 'L0_tok_W_h2e': _L0_tok_in['W_h2e'], 'L0_tok_b_h2e': _L0_tok_in['b_h2e'], 'L0_attn_Wq1': _L0_attn_in['Wq1'], 'L0_attn_Wk1': _L0_attn_in['Wk1'], 'L0_attn_Wq2': _L0_attn_in['Wq2'], 'L0_attn_Wk2': _L0_attn_in['Wk2'], 'L0_attn_Wv': _L0_attn_in['Wv'], 'L0_attn_Wo': _L0_attn_in['Wo'], 'L0_attn_gw1': _L0_attn_in['gw1'], 'L0_attn_gb1': _L0_attn_in['gb1'], 'L0_attn_gw2': _L0_attn_in['gw2'], 'L0_attn_gb2': _L0_attn_in['gb2'], 'L0_attn_gw3': _L0_attn_in['gw3'], 'L0_attn_gb3': _L0_attn_in['gb3'], 'L0_ffn_ln_g': _L0_ffn_in['ln_g'], 'L0_ffn_ln_b': _L0_ffn_in['ln_b'], 'L0_ffn_attn_w': _L0_ffn_in['attn_w'], 'L0_ffn_attn_b': _L0_ffn_in['attn_b'], 'L0_ffn_gate_w': _L0_ffn_in['gate_w'], 'L0_ffn_fc1_w': _L0_ffn_in['fc1_w'], 'L0_ffn_fc1_b': _L0_ffn_in['fc1_b'], 'L0_ffn_fc2_w': _L0_ffn_in['fc2_w'], 'L0_ffn_fc2_b': _L0_ffn_in['fc2_b'], 'L0_ffn_next_w': _L0_ffn_in['next_w'], 'L0_ffn_next_b': _L0_ffn_in['next_b']}

def reference(x, L0_tok_emb_table, L0_tok_W_e2h, L0_tok_b_e2h, L0_tok_conv_w, L0_tok_conv_b, L0_tok_W_h2e, L0_tok_b_h2e, L0_attn_Wq1, L0_attn_Wk1, L0_attn_Wq2, L0_attn_Wk2, L0_attn_Wv, L0_attn_Wo, L0_attn_gw1, L0_attn_gb1, L0_attn_gw2, L0_attn_gb2, L0_attn_gw3, L0_attn_gb3, L0_ffn_ln_g, L0_ffn_ln_b, L0_ffn_attn_w, L0_ffn_attn_b, L0_ffn_gate_w, L0_ffn_fc1_w, L0_ffn_fc1_b, L0_ffn_fc2_w, L0_ffn_fc2_b, L0_ffn_next_w, L0_ffn_next_b):
    import jax
    import jax.numpy as jnp

    def _L0_tok_ref(src, emb_table, W_e2h, b_e2h, conv_w, conv_b, W_h2e, b_h2e):
        import jax, jax.numpy as jnp
        import numpy as np
        VOCAB = 3750
        EMB = 128
        HID = 128
        N_LAYERS = 6
        KSIZE = 3
        SCALE = 0.7071067811865476

        def _conv1d_same(x, w, b):
            y = jax.lax.conv_general_dilated(x, w, window_strides=(1,), padding='SAME', dimension_numbers=('NCH', 'OIH', 'NCH'))
            return y + b[None, :, None]
        embedded = emb_table[src]
        h = embedded @ W_e2h + b_e2h
        x = jnp.transpose(h, (0, 2, 1))
        for i in range(N_LAYERS):
            conved = _conv1d_same(x, conv_w[i], conv_b[i])
            a, g = jnp.split(conved, 2, axis=1)
            glu = a * jax.nn.sigmoid(g)
            x = (glu + x) * SCALE
        out = jnp.transpose(x, (0, 2, 1)) @ W_h2e + b_h2e
        return out

    def _L0_attn_ref(x, Wq1, Wk1, Wq2, Wk2, Wv, Wo, gw1, gb1, gw2, gb2, gw3, gb3):
        import jax, jax.numpy as jnp
        import numpy as np
        B, L, D, H = (4, 256, 128, 8)
        HD = D // H

        def _window_size(L):
            for cand in (5, 4, 3, 2):
                if L % cand == 0:
                    return cand
            return 5

        def _window_stats(attn, ws):
            b, h, l, _ = attn.shape
            nw = l // ws
            r = attn.reshape(b, h, nw, ws, l)
            mean = r.mean(axis=(-1, -2))
            std = jnp.std(r, axis=-1, ddof=1).mean(axis=-1)
            mx = r.max(axis=-1).mean(axis=-1)
            mn = r.min(axis=-1).mean(axis=-1)
            return jnp.stack([mean, std, mx, mn], axis=-1)
        b, l, d = x.shape
        hd = d // H
        scale = 1.0 / jnp.sqrt(jnp.float32(hd))

        def heads(y):
            return y.reshape(b, l, H, hd).transpose(0, 2, 1, 3)
        q1, k1 = (heads(x @ Wq1), heads(x @ Wk1))
        q2, k2 = (heads(x @ Wq2), heads(x @ Wk2))
        v = heads(x @ Wv)
        attn1 = jax.nn.softmax(jnp.einsum('bhqd,bhkd->bhqk', q1, k1) * scale, axis=-1)
        attn2 = jax.nn.softmax(jnp.einsum('bhqd,bhkd->bhqk', q2, k2) * scale, axis=-1)
        ws = _window_size(l)
        gate_in = jnp.concatenate([_window_stats(attn1, ws), _window_stats(attn2, ws)], axis=-1)
        hid = jax.nn.relu(gate_in @ gw1 + gb1)
        hid = jax.nn.relu(hid @ gw2 + gb2)
        alpha = jax.nn.sigmoid(hid @ gw3 + gb3)
        alpha_full = jnp.repeat(alpha, ws, axis=2)
        fused = alpha_full * attn1 + (1.0 - alpha_full) * attn2
        out = jnp.einsum('bhqk,bhkd->bhqd', fused, v)
        out = out.transpose(0, 2, 1, 3).reshape(b, l, d)
        return out @ Wo

    def _L0_ffn_ref(x, ln_g, ln_b, attn_w, attn_b, gate_w, fc1_w, fc1_b, fc2_w, fc2_b, next_w, next_b):
        import jax, jax.numpy as jnp
        import numpy as np
        MICRO_BATCHES = 2
        TOP_K = 2
        D = 128
        E = 8
        B, S = (8, 2048)
        b, s, d = x.shape
        xf = x.reshape(b * s, d)
        mu = jnp.mean(xf, axis=-1, keepdims=True)
        var = jnp.var(xf, axis=-1, keepdims=True)
        normed = (xf - mu) / jnp.sqrt(var + 1e-05) * ln_g + ln_b
        x_attn = normed @ attn_w.T + attn_b + xf
        logits = x_attn @ gate_w.T
        _scores, _indices = jax.lax.top_k(logits, TOP_K)
        e = fc1_w.shape[0]
        t = b * s // (MICRO_BATCHES * e)
        tok = x_attn.reshape(MICRO_BATCHES, e, t, d)
        h = jnp.einsum('meti,ehi->meth', tok, fc1_w) + fc1_b[None, :, None, :]
        h = jax.nn.gelu(h, approximate=False)
        y = jnp.einsum('meth,edh->metd', h, fc2_w) + fc2_b[None, :, None, :]
        yf = y.reshape(b * s, d)
        out = jax.nn.gelu(yf @ next_w.T + next_b, approximate=False)
        return out.reshape(b, s, d)
    h = _L0_tok_ref(x, L0_tok_emb_table, L0_tok_W_e2h, L0_tok_b_e2h, L0_tok_conv_w, L0_tok_conv_b, L0_tok_W_h2e, L0_tok_b_h2e)
    h = h + _L0_attn_ref(_layernorm(h, axis=-1), L0_attn_Wq1, L0_attn_Wk1, L0_attn_Wq2, L0_attn_Wk2, L0_attn_Wv, L0_attn_Wo, L0_attn_gw1, L0_attn_gb1, L0_attn_gw2, L0_attn_gb2, L0_attn_gw3, L0_attn_gb3)
    h = h + _L0_ffn_ref(_layernorm(h, axis=-1), L0_ffn_ln_g, L0_ffn_ln_b, L0_ffn_attn_w, L0_ffn_attn_b, L0_ffn_gate_w, L0_ffn_fc1_w, L0_ffn_fc1_b, L0_ffn_fc2_w, L0_ffn_fc2_b, L0_ffn_next_w, L0_ffn_next_b)
    return h

_drawn_inputs = setup_inputs


def setup_inputs(seed=0):
    import zlib

    import numpy as np

    out = dict(_drawn_inputs(seed))
    spreads = {'L0_tok_b_e2h': (0.0, 0.1),
     'L0_tok_conv_b': (0.0, 0.1),
     'L0_tok_b_h2e': (0.0, 0.1),
     'L0_attn_gb1': (0.0, 2.0),
     'L0_attn_gb2': (0.0, 2.0),
     'L0_ffn_ln_g': (1.0, 0.6),
     'L0_ffn_ln_b': (0.0, 0.8),
     'L0_ffn_attn_b': (0.0, 0.8),
     'L0_ffn_fc1_b': (0.0, 0.364),
     'L0_ffn_fc2_b': (0.0, 0.1),
     'L0_ffn_next_b': (0.0, 0.1)}
    factors = {'L0_tok_emb_table': 8.0,
     'L0_tok_W_e2h': 8.0,
     'L0_tok_conv_w': 3.741,
     'L0_attn_Wq1': 200.0,
     'L0_attn_Wk1': 200.0,
     'L0_attn_Wq2': 64.0,
     'L0_attn_Wk2': 64.0,
     'L0_attn_gw1': 64.0,
     'L0_attn_gw2': 200.0,
     'L0_attn_gw3': 64.0,
     'L0_ffn_attn_w': 4.293}
    for name, (base, spread) in spreads.items():
        noise = np.random.default_rng([zlib.crc32(name.encode()), seed]).standard_normal(out[name].shape)
        drawn = base * np.exp(spread * noise) if base else spread * noise
        out[name] = jnp.asarray(drawn.astype(out[name].dtype))
    for name, factor in factors.items():
        out[name] = (out[name] * factor).astype(out[name].dtype)
    return out
```

```python
from contextlib import ExitStack

import numpy as np

import concourse.bass as bass
from concourse import mybir

F32 = mybir.dt.float32
BF16 = mybir.dt.bfloat16
I32 = mybir.dt.int32
ALU = mybir.AluOpType
ACT = mybir.ActivationFunctionType
AX = mybir.AxisListType.X

P = 128
L = 1024
T = L // P
H = 8
HD = P // H
VW = HD + 1
U = 2 * H
STEPS = U * T
E = 8
FC = 4
WS = 4
NW = P // WS
LAYERS, TAPS = 6, 3
RING = 4
NPART = 6
KSC = NPART * HD
KST = KSC + 3
Q_PART = (0, 0, 0, 1, 1, 2)
K_PART = (0, 1, 2, 0, 1, 0)
LAG_T = T + 2
LAG_V = LAG_T + 2
CH = 256
NC = L // CH
RES = 0.7071067811865476
EPS = 1e-5

GATE = [("snap",), ("win",), ("hid1",), ("hid2",), ("logit",), ("alpha",)]


def two(kind):
    return [(kind, 0), (kind, 1)]


CONV = [("conv" + half, l, c) for l in range(LAYERS) for c in range(NC) for half in "ag"]
QK = [[("qk", a, w, k) for w in range(2) for k in range(2)] for a in range(2)]
PRE = [("gather",)] + two("embT") + two("e2h") + CONV + two("h2e") + [("ln1",)] + two("xnT") + QK[0] + two("v")
POST = ([("snap",), ("win",), ("hid1",), ("hid2",), ("logit",), ("alpha",)] + two("attT") + two("wo")
        + [("ln2",), ("ln3",)] + two("nT") + [("attw", c) for c in range(NC)]
        + [("fc1", c, j) for c in range(NC) for j in range(2)] + [("gelu1",)]
        + [("fc2", c) for c in range(NC)] + two("next") + [("gelu2",)])
ENGINES = {
    "mrow": ("pool", "pe", "act"), "vcopy": ("pool",), "hcopy": ("pool",), "snap": ("pool", "act"),
    "win": ("pe", "dve"), "hid1": ("pe", "dve"), "hid2": ("pe", "dve"), "logit": ("pe", "act", "pool"),
    "alpha": ("pe", "dve", "pool"), "attT": ("pe", "act"), "wo": ("pe", "dve"), "ln2": ("dve", "pool"),
    "ln3": ("dve", "pool"), "nT": ("pe", "act"), "attw": ("pe", "act"), "fc1": ("pe", "act"), "gelu1": ("act",),
    "fc2": ("pe", "act"), "next": ("pe", "dve"), "gelu2": ("act", "pool"), "gather": (), "embT": ("pe", "act"),
    "e2h": ("pe", "act"), "conva": ("pe", "act"), "convg": ("pe", "act", "pool"), "h2e": ("pe", "dve"),
    "ln1": ("dve", "pool"), "xnT": ("pe", "act"), "qk": ("pe", "act", "pool"), "v": ("pe", "dve"),
}
READER = {k: ("dve" if "dve" in v else "act") for k, v in ENGINES.items() if "pe" in v}


def plan():
    at = {n: [] for n in range(STEPS)}
    for j in range(U):
        at[j * T].append(("mrow", j))
    fixed = {3: [("vcopy", 0)], 12: [("vcopy", 1)], 1: [QK[1][0]], 2: [QK[1][1]], 4: [QK[1][2]], 5: [QK[1][3]],
             13: [("snap",)], 14: [("win",)], 15: [("hid1",)], 17: [("hid2",)], 18: [("logit",)], 19: [("alpha",)],
             21: [("attT", 0)], 22: [("attT", 1)], 23: [("wo", 0), ("wo", 1)], 25: [("hcopy",), ("ln2",)],
             27: [("ln3",)], 20: [("gather",)]}
    for n, tasks in fixed.items():
        at[n] += tasks
    rest = POST[POST.index(("nT", 0)):]
    n = 30
    for task in rest:
        at[n].append(task)
        n += 1
    n += 1
    for task in PRE[1:]:
        at[n].append(task)
        n += 2 if task[0] in ("ln1",) else 1
    assert n <= STEPS - T, n
    return at


STEP = plan()
BODY = [task for n in range(STEPS) for task in STEP[n]]
TAIL = [("mrow", 0)] + POST
PHASES = {"pre": PRE, "body": BODY, "tail": TAIL}


class Side:

    def __init__(self, sems):
        self.sems = sems

    def upto(self, phase, i, eng, task):
        tasks = PHASES[phase]
        n = 0 if task is None else tasks.index(task) + 1
        count = sum(eng in ENGINES[t[0]] for t in tasks[:n])
        if phase == "pre":
            return count
        count += sum(eng in ENGINES[t[0]] for t in PRE)
        return i * sum(eng in ENGINES[t[0]] for t in BODY) + count


def tower_kernel(nc, ids, table, consts, w_e2h, b_e2h, conv_w, conv_b, w_h2e, b_h2e, wq1, wk1, wq2, wk2, wv, wo,
                 gw1, gb1, gw2, gb2, gw3, gb3, ln_g, ln_b, attn_w, attn_b, fc1_w, fc1_b, fc2_w, fc2_b,
                 next_w, next_b, out):
    NB = ids.shape[0] - 1

    with ExitStack() as ctx:
        def sb(name, shape, dt=F32):
            return ctx.enter_context(nc.sbuf_tensor(name, shape, dt))

        def sem(name):
            return ctx.enter_context(nc.semaphore(name))

        ps_s = ctx.enter_context(nc.psum_tensor("ps_s", [P, 2, L], F32))
        ps_t = ctx.enter_context(nc.psum_tensor("ps_t", [P, 2, 512], F32))
        ps_o = ctx.enter_context(nc.psum_tensor("ps_o", [P, 512], F32))
        ps_w = ctx.enter_context(nc.psum_tensor("ps_w", [P, 512], F32))

        cst = sb("cst", [P, P + NW + P])
        ident = cst[:, 0:P]
        win_mean = cst[:, P:P + NW]
        win_rep = cst[0:NW, P + NW:P + NW + P]
        ident_b = sb("ident_b", [P, P], BF16)
        cw = sb("cw", [P, LAYERS, TAPS, 2 * P])
        cb = sb("cb", [P, 2 * LAYERS])
        cb_half = sb("cb_half", [P, 2 * LAYERS])
        we2h, wh2e = sb("we2h", [P, P]), sb("wh2e", [P, P])
        wqk = sb("wqk", [P, 2, 2, P])
        wv_s, wo_s, wattn, wnext = sb("wv_s", [P, P]), sb("wo_s", [P, P]), sb("wattn", [P, P]), sb("wnext", [P, P])
        col = sb("col", [P, 2])
        row = sb("row", [P, 4, P])
        g1 = sb("g1", [H * 8, 2, P])
        g2 = sb("g2", [P, 4 * HD])
        g3 = sb("g3", [4 * HD, 4])
        g1b, g2b = sb("g1b", [P, 1]), sb("g2b", [4 * HD, 1])
        g3b, g3h = sb("g3b", [NW, 1]), sb("g3h", [NW, 1])
        half_pow = sb("half_pow", [P, H * T])
        rs_pow = sb("rs_pow", [P, T])

        part = sb("part", [P, 2, 2, 3, L], BF16)
        qst = sb("qst", [KST, RING, L], BF16)
        kst = sb("kst", [KST, RING, L], BF16)
        exps = sb("exps", [P, RING, L])
        junk = sb("junk", [P, 2, L], BF16)
        negmax, rowmin, sumsq = (sb(n, [P, RING, T]) for n in ("negmax", "rowmin", "sumsq"))
        mparts = sb("mparts", [P, 3, T], BF16)
        mrest = sb("mrest", [P, 2, T])
        mrow = sb("mrow", [3 * T, P], BF16)
        v_next, v_cur = sb("v_next", [P, T, H * VW]), sb("v_cur", [P, T, H * VW])
        o_all = sb("o_all", [P, U, T, HD])
        recip, mean_all, sq_all, dif_all = (sb(n, [P, U, T]) for n in ("recip", "mean_all", "sq_all", "dif_all"))

        gin = sb("gin", [P, T, H, 8])
        gtmp = sb("gtmp", [P, 4, U * T])
        winm = sb("winm", [H * 8, T * NW])
        hid1 = sb("hid1", [P, 2, T * NW])
        hid2 = sb("hid2", [4 * HD, 2, T * NW])
        alpha_w = sb("alpha_w", [NW, 2, T * H])
        alpha_q = sb("alpha_q", [P, T * H])
        odif, o2 = sb("odif", [P, T, P]), sb("o2", [P, T, P])
        att = sb("att", [P, T, P])
        chan = sb("chan", [P, L])
        h_next, h_cur, h2 = sb("h_next", [P, T, P]), sb("h_cur", [P, T, P]), sb("h2", [P, T, P])
        x2 = sb("x2", [P, T, P])
        bn = sb("bn", [P, T, 6])
        mv = sb("mv", [P, 3, T, 2])
        rstd = sb("rstd", [P, 3, T])
        xa = sb("xa", [P, L])
        hpre = sb("hpre", [P, FC, L])
        y = chan
        z = sb("z", [P, T, P])
        fc1s, fc2s = sb("fc1s", [P, FC * P]), sb("fc2s", [P, FC, P])
        fc1bs, fc2bs = sb("fc1bs", [P, FC]), sb("fc2bs", [P, 1])

        idx = sb("idx", [P, T], I32)
        xc = sb("xc", [P, 2, L + 2])
        va, ug = sb("va", [P, 2, CH]), sb("ug", [P, 2, CH])
        ctmp = sb("ctmp", [P, 4, CH])
        xn = sb("xn", [P, T, P])
        xn_t = sb("xn_t", [P, L])
        emb, emb_t = xn, xn_t
        stage = sb("stage", [P, 2, 512])
        srest = sb("srest", [P, 512])

        s_load = sem("s_load")
        s_init = sem("s_init")
        s_scores = sem("s_scores")
        s_max = sem("s_max")
        s_min = sem("s_min")
        s_sq = sem("s_sq")
        s_st = sem("s_st")
        s_exp = sem("s_exp")
        s_pv = sem("s_pv")
        s_o = sem("s_o")
        s_stat = sem("s_stat")
        s_ring = [sem(f"s_ring{r}") for r in range(RING)]
        s_mrow = sem("s_mrow")
        s_idx = sem("s_idx")
        s_emb = sem("s_emb")
        s_exw = sem("s_exw")
        s_out = sem("s_out")
        s_dchain = sem("s_dchain")
        s_pchain = sem("s_pchain")
        side_sem = {e: sem("side_" + e) for e in ("pe", "act", "dve", "pool")}
        side = Side(side_sem)

        def wait_side(eng, phase, i, of, task=None):
            eng.wait_ge(side_sem[of], side.upto(phase, i, of, task))

        def wait_bank(eng, phase, i, task):
            tasks = PHASES[phase]
            before = [t for t in tasks[:tasks.index(task)] if t[0] in READER]
            if before:
                wait_side(eng, phase, i, READER[before[-1][0]], before[-1])
            elif phase == "body":
                wait_side(eng, phase, i, "act")
                wait_side(eng, phase, i, "dve")
            elif phase == "tail":
                wait_side(eng, phase, i, "act")
                wait_side(eng, phase, i, "dve")

        def wait_own(eng, phase, i, name, task):
            tasks = PHASES[phase]
            before = [t for t in tasks[:tasks.index(task)] if name in ENGINES[t[0]]]
            if before or phase != "pre":
                wait_side(eng, phase, i, name, before[-1] if before else None)

        def setup_loads(eng):
            n = 0
            pairs = [(cst[:, :], consts), (cw[:, :, :, :], conv_w), (cb[:, :], conv_b), (we2h[:, :], w_e2h),
                     (wh2e[:, :], w_h2e), (wqk[:, 0, 0, :], wq1), (wqk[:, 0, 1, :], wk1), (wqk[:, 1, 0, :], wq2),
                     (wqk[:, 1, 1, :], wk2), (wv_s[:, :], wv), (wo_s[:, :], wo), (wattn[:, :], attn_w),
                     (wnext[:, :], next_w), (col[:, 0:1], b_e2h), (col[:, 1:2], attn_b)]
            for k, b in enumerate((b_h2e, next_b, ln_g, ln_b)):
                pairs.append((row[:, k, :], b.to_broadcast([P, P])))
            for h in range(H):
                pairs.append((g1[8 * h:8 * h + 8, h // 4, 32 * (h % 4):32 * (h % 4) + 32], gw1))
            for j in range(4):
                pairs.append((g2[32 * j:32 * j + 32, HD * j:HD * j + HD], gw2))
                pairs.append((g3[HD * j:HD * j + HD, j:j + 1], gw3))
                pairs.append((g1b[32 * j:32 * j + 32, :], gb1))
                pairs.append((g2b[HD * j:HD * j + HD, :], gb2))
            pairs.append((g3b[:, :], gb3.to_broadcast([NW, 1])))
            for dst, src in pairs:
                eng.dma_start(dst, src).then_inc(s_load, 16)
                n += 1
            return n

        N_LOADS = 15 + 4 + H + 16 + 1

        block = ctx.enter_context(nc.Block())

        @block.sync
        def _(sp):
            def settle():
                sp.nop(nofuse=True)

            sp.wait_ge(s_init, 1)
            assert setup_loads(sp) == N_LOADS

            def load_ids(b):
                sp.dma_start(idx[:, :], ids[b]).then_inc(s_idx, 16)

            def load_unit(u):
                a, h, r = u // H, u % H, u % RING
                for g in range(NPART):
                    for dst, w, c in ((qst, 0, Q_PART[g]), (kst, 1, K_PART[g])):
                        sp.dma_start(dst[HD * g:HD * g + HD, r, :], part[HD * h:HD * h + HD, a, w, c, :])\
                          .then_inc(s_ring[r], 16)

            def store_mrow(phase, i, j):
                wait_side(sp, phase, i, "act", ("mrow", j))
                settle()
                for c in range(3):
                    sp.dma_start(qst[KSC + c:KSC + c + 1, (j - 1) % RING, :].rearrange("o (t q) -> o t q", t=T),
                                 mrow[T * c:T * c + T, :]).then_inc(s_mrow, 16)

            def load_expert(phase, i, e):
                wait_side(sp, phase, i, "pe")
                settle()
                wait_side(sp, phase, i, "act")
                settle()
                for dst, src in ((fc1s[:, :], fc1_w[e]), (fc2s[:, :, :], fc2_w[e]), (fc1bs[:, :], fc1_b[e]),
                                 (fc2bs[:, :], fc2_b[e])):
                    sp.dma_start(dst, src).then_inc(s_exw, 16)

            def store_out(phase, i):
                wait_side(sp, phase, i, "pool", ("gelu2",))
                settle()
                sp.dma_start(out[i], z[:, :, :]).then_inc(s_out, 16)

            load_ids(0)
            wait_side(sp, "pre", 0, "pool", QK[0][-1])
            load_unit(0)
            with sp.Fori(0, NB // E) as group, sp.Fori(0, E) as e:
                i = group * E + e
                sp.wait_ge(s_emb, i * (16 * T) + 16 * T)
                settle()
                load_ids(i + 1)
                load_expert("body", i, e)
                for j in range(U):
                    if j:
                        sp.wait_ge(s_st, i * (2 * STEPS) + 2 * (T * (j - 3) + T - 1 + LAG_T) + 2)
                    else:
                        sp.wait_ge(s_exp, i * (2 * STEPS) + 2)
                    settle()
                    if j + 1 in (U // 2, U):
                        wait_side(sp, "body", i, "pool", QK[(j + 1) % U // H][-1])
                        settle()
                    store_mrow("body", i, j)
                    load_unit((j + 1) % U)
                    if ("gelu2",) in sum((STEP[n] for n in range(j * T, j * T + T)), []):
                        store_out("body", i)
            load_expert("tail", NB, 0)
            store_mrow("tail", NB, 0)
            store_out("tail", NB)
            sp.wait_ge(s_out, 16 * (NB + 2))

        @block.tensor
        def _(pe):
            def mm(dst, lhs, rhs, start=True, stop=True, **kw):
                return nc.tensor.matmul(dst, lhs, rhs, start=start, stop=stop, **kw)

            def scores(i, n):
                u, t = n // T, n % T
                if t == 0:
                    pe.wait_ge(s_ring[u % RING], i * (4 * 12 * 16) + 12 * 16 * (u // RING + 1))
                pe.wait_ge(s_min, i * STEPS + n + 1)
                for c in range(2):
                    last = mm(ps_s[:, n % 2, 512 * c:512 * c + 512], qst[0:KSC, u % RING, P * t:P * t + P],
                              kst[0:KSC, u % RING, 512 * c:512 * c + 512])
                last.then_inc(s_scores, 1)

            def scores_t(i, n):
                m = (n - LAG_T) % STEPS
                u, t = m // T, m % T
                if t == 0:
                    pe.wait_ge(s_mrow, i * (U * 48) + 48 * (n // T + 2))
                for c in range(2):
                    pe.wait_ge(s_exp, i * (2 * STEPS) + 2 * n + c + 1)
                    mm(ps_t[:, c, :], kst[:, u % RING, P * t:P * t + P], qst[:, u % RING, 512 * c:512 * c + 512])\
                        .then_inc(s_st, 1)

            def weighted(i, n, count=True):
                m = (n - LAG_V) % STEPS
                h, t = m // T % H, m % T
                if count:
                    pe.wait_ge(s_exp, i * (2 * STEPS) + max(2 * n, 1))
                    if t == 0:
                        pe.wait_ge(s_o, i * U + n // T + 1)
                    if m == 0:
                        wait_side(pe, "body", i, "pool", ("vcopy", 0))
                    if m == 6 * T:
                        wait_side(pe, "body", i, "pool", ("vcopy", 1))
                for q in range(T):
                    last = mm(ps_o[:, VW * q:VW * q + VW], exps[:, (n - 2) % RING, P * q:P * q + P],
                              v_cur[:, t, VW * h:VW * h + VW], start=(t == 0 and q == 0), stop=(t == T - 1),
                              skip_group_check=True)
                if count:
                    last.then_inc(s_pv, 1)

            def turn(src, k):
                for q in range(4):
                    last = nc.tensor.transpose(ps_w[:, P * q:P * q + P], src[:, 4 * k + q, :], ident)
                return last

            def task(phase, i, tk):
                kind = tk[0]
                if "pe" not in ENGINES[kind]:
                    return
                wait_bank(pe, phase, i, tk)
                w = lambda of, t: wait_side(pe, phase, i, of, t)
                if kind == "mrow":
                    w("pool", tk)
                    last = nc.tensor.transpose(ps_w[0:3 * T, 0:P // 2].bitcast(BF16),
                                               mparts[:, :, :].rearrange("p c t -> p (c t)"), ident_b[:, :])
                elif kind == "win":
                    w("pool", ("snap",))
                    for t in range(T):
                        last = mm(ps_w[0:H * 8, NW * t:NW * t + NW], gin[:, t, :, :].rearrange("p h f -> p (h f)"),
                                  win_mean)
                elif kind == "hid1":
                    w("dve", ("win",))
                    for g in range(2):
                        last = mm(ps_w[:, CH * g:CH * g + CH], g1[:, g, :], winm[:, :])
                elif kind == "hid2":
                    w("dve", ("hid1",))
                    for g in range(2):
                        last = mm(ps_w[0:4 * HD, CH * g:CH * g + CH], g2[:, :], hid1[:, g, :])
                elif kind == "logit":
                    w("dve", ("hid2",))
                    pe.nop(nofuse=True)
                    for t in range(T):
                        for g in range(2):
                            last = mm(ps_w[0:NW, H * t + 4 * g:H * t + 4 * g + 4],
                                      hid2[:, g, NW * t:NW * t + NW], g3[:, :])
                elif kind == "alpha":
                    w("pool", ("logit",))
                    last = mm(ps_w[:, 0:T * H], win_rep, alpha_w[:, 1, :])
                elif kind == "attT":
                    w("pool", ("alpha",))
                    last = turn(att, tk[1])
                elif kind == "wo":
                    w("act", ("attT", tk[1]))
                    for q in range(4):
                        t = 4 * tk[1] + q
                        last = mm(ps_w[:, P * q:P * q + P], chan[:, P * t:P * t + P], wo_s[:, :])
                elif kind == "nT":
                    w("pool", ("ln3",))
                    last = turn(att, tk[1])
                elif kind == "attw":
                    c = tk[1]
                    w("act", ("nT", c // 2))
                    mm(ps_w[:, 0:CH], wattn[:, :], chan[:, CH * c:CH * c + CH], stop=False, skip_group_check=True)
                    for q in range(2):
                        last = mm(ps_w[:, P * q:P * q + P], x2[:, 2 * c + q, :], ident, start=False,
                                  skip_group_check=True)
                elif kind == "fc1":
                    _, c, j = tk
                    if (c, j) == (0, 0):
                        pe.wait_ge(s_exw, i * 64 + 64)
                    w("act", ("attw", c))
                    for q in range(2):
                        f = 2 * j + q
                        last = mm(ps_w[:, CH * q:CH * q + CH], fc1s[:, P * f:P * f + P], xa[:, CH * c:CH * c + CH])
                elif kind == "fc2":
                    c = tk[1]
                    w("act", ("gelu1",))
                    for f in range(FC):
                        last = mm(ps_w[:, 0:CH], fc2s[:, f, :], hpre[:, f, CH * c:CH * c + CH], start=(f == 0),
                                  stop=(f == FC - 1))
                elif kind == "next":
                    w("act", ("fc2", 2 * tk[1] + 1))
                    for q in range(4):
                        t = 4 * tk[1] + q
                        last = mm(ps_w[:, P * q:P * q + P], y[:, P * t:P * t + P], wnext[:, :])
                elif kind == "embT":
                    pe.wait_ge(s_emb, (16 * T) if phase == "pre" else (i + 2) * (16 * T))
                    last = turn(emb, tk[1])
                elif kind == "e2h":
                    w("act", ("embT", tk[1]))
                    last = mm(ps_w[:, :], we2h[:, :], emb_t[:, 512 * tk[1]:512 * tk[1] + 512])
                elif kind in ("conva", "convg"):
                    _, l, c = tk
                    if l == 0:
                        w("act", ("e2h", min((CH * c + CH) // 512, 1)))
                    else:
                        w("pool", ("convg", l - 1, min(c + 1, NC - 1)))
                    g = kind == "convg"
                    for k in range(TAPS):
                        last = mm(ps_w[:, CH * g:CH * g + CH], cw[:, l, k, P * g:P * g + P],
                                  xc[:, l % 2, CH * c + k:CH * c + k + CH], start=(k == 0), stop=(k == TAPS - 1))
                elif kind == "h2e":
                    w("pool", ("convg", LAYERS - 1, NC - 1))
                    for q in range(4):
                        t = 4 * tk[1] + q
                        last = mm(ps_w[:, P * q:P * q + P], xc[:, 0, 1 + P * t:1 + P * t + P], wh2e[:, :])
                elif kind == "xnT":
                    w("pool", ("ln1",))
                    last = turn(xn, tk[1])
                elif kind == "qk":
                    _, a, which, k = tk
                    if a == 0:
                        w("act", ("xnT", k))
                    last = mm(ps_w[:, :], wqk[:, a, which, :], xn_t[:, 512 * k:512 * k + 512])
                elif kind == "v":
                    w("act", ("xnT", tk[1]))
                    for q in range(4):
                        t = 4 * tk[1] + q
                        last = mm(ps_w[:, P * q:P * q + P], xn_t[:, P * t:P * t + P], wv_s[:, :])
                last.then_inc(side_sem["pe"], 1)

            pe.wait_ge(s_load, 16 * N_LOADS)
            pe.wait_ge(s_init, 3)
            for n in range(-((-LAG_V) % T), 0):
                weighted(0, n, count=False)
            for tk in PRE:
                task("pre", 0, tk)
            with pe.Fori(0, NB // E) as group, pe.Fori(0, E) as e:
                i = group * E + e
                for n in range(0, STEPS, 2):
                    for k in (n, n + 1):
                        scores(i, k)
                        scores_t(i, k)
                    for k in (n, n + 1):
                        for tk in STEP[k]:
                            task("body", i, tk)
                        weighted(i, k)
            task("tail", NB, TAIL[0])
            for n in range(LAG_V):
                if n < LAG_T:
                    scores_t(NB, n)
                weighted(NB, n)
            for tk in TAIL[1:]:
                task("tail", NB, tk)

        @block.scalar
        def _(act):
            def squares(i, n):
                r, t = n // T % RING, n % T
                if t == 0:
                    act.wait_ge(s_stat, i * U + n // T + 1)
                act.wait_ge(s_max, i * STEPS + n + 1)
                act.wait_ge(s_sq, i * STEPS + n + 1)
                nc.scalar.activation(junk[:, n % 2, :], ps_s[:, n % 2, :], ACT.Exp, bias=negmax[:, r, t:t + 1],
                                     accum_out=sumsq[:, r, t:t + 1]).then_inc(s_sq, 1)

            def exp_t(i, n):
                act.wait_ge(s_pv, i * STEPS + n + 1)
                for c in range(2):
                    act.wait_ge(s_st, i * (2 * STEPS) + 2 * n + c + 1)
                    nc.scalar.activation(exps[:, n % RING, 512 * c:512 * c + 512], ps_t[:, c, :], ACT.Exp,
                                         scale=0.5).then_inc(s_exp, 1)

            def ident_act(dst, src, **kw):
                return nc.scalar.activation(dst, src, ACT.Identity, **kw)

            def copy(dst, src):
                return nc.scalar.activation(dst, src, ACT.Copy)

            def task(phase, i, tk):
                kind = tk[0]
                if "act" not in ENGINES[kind]:
                    return
                w = lambda of, t: wait_side(act, phase, i, of, t)
                if "pe" in ENGINES[kind]:
                    w("pe", tk)
                if kind == "mrow":
                    j = tk[1]
                    act.wait_ge(s_mrow, i * (U * 48) + 48 * (j + 1))
                    last = copy(mrow[:, :], ps_w[0:3 * T, 0:P // 2].bitcast(BF16))
                elif kind == "snap":
                    act.wait_ge(s_stat, i * U + 3)
                    last = nc.scalar.activation(gtmp[:, 0, :], dif_all[:, :, :].rearrange("p u t -> p (u t)"),
                                                ACT.Exp, scale=0.5)
                elif kind == "logit":
                    last = nc.scalar.activation(alpha_w[:, 0, :], ps_w[0:NW, 0:T * H], ACT.Tanh, bias=g3h[:, :],
                                                scale=0.5)
                elif kind in ("attT", "nT"):
                    last = copy(chan[:, 512 * tk[1]:512 * tk[1] + 512], ps_w[:, :])
                elif kind == "attw":
                    last = ident_act(xa[:, CH * tk[1]:CH * tk[1] + CH], ps_w[:, 0:CH], bias=col[:, 1:2])
                elif kind == "fc1":
                    _, c, j = tk
                    if (c, j) == (0, 0):
                        act.wait_ge(s_exw, i * 64 + 64)
                    for q in range(2):
                        f = 2 * j + q
                        last = ident_act(hpre[:, f, CH * c:CH * c + CH], ps_w[:, CH * q:CH * q + CH],
                                         bias=fc1bs[:, f:f + 1])
                elif kind == "gelu1":
                    w("act", ("fc1", NC - 1, 1))
                    for f in range(FC):
                        last = nc.scalar.activation(hpre[:, f, :], hpre[:, f, :], ACT.Gelu)
                elif kind == "fc2":
                    last = ident_act(y[:, CH * tk[1]:CH * tk[1] + CH], ps_w[:, 0:CH], bias=fc2bs[:, :])
                elif kind == "gelu2":
                    w("dve", ("next", 1))
                    last = nc.scalar.activation(z[:, :, :], z[:, :, :], ACT.Gelu)
                elif kind == "embT":
                    last = copy(emb_t[:, 512 * tk[1]:512 * tk[1] + 512], ps_w[:, :])
                elif kind == "e2h":
                    if tk[1] == 0:
                        w("pool", None)
                    last = ident_act(xc[:, 0, 1 + 512 * tk[1]:513 + 512 * tk[1]], ps_w[:, :], bias=col[:, 0:1])
                elif kind in ("conva", "convg"):
                    _, l, c = tk
                    k = CONV.index(tk) // 2
                    if kind == "conva" and k >= 2:
                        w("pool", CONV[2 * (k - 2) + 1])
                    if kind == "conva":
                        last = ident_act(va[:, c % 2, :], ps_w[:, 0:CH], bias=cb[:, 2 * l:2 * l + 1])
                    else:
                        last = nc.scalar.activation(ug[:, c % 2, :], ps_w[:, CH:2 * CH], ACT.Tanh, scale=0.5,
                                                    bias=cb_half[:, 2 * l + 1:2 * l + 2])
                elif kind == "xnT":
                    last = copy(xn_t[:, 512 * tk[1]:512 * tk[1] + 512], ps_w[:, :])
                elif kind == "qk":
                    _, a, which, k = tk
                    at = QK[a].index(tk)
                    if at >= 2:
                        w("pool", QK[a][at - 2])
                    elif phase == "body":
                        w("pool", None)
                    last = ident_act(stage[:, k, :], ps_w[:, :], scale=0.5 if which == 0 else 1.0)
                last.then_inc(side_sem["act"], 1)

            act.wait_ge(s_load, 16 * N_LOADS)
            act.wait_ge(s_init, 3)
            nc.scalar.activation(g3h[:, :], g3b[:, :], ACT.Copy, scale=0.5)
            nc.scalar.activation(cb_half[:, :], cb[:, :], ACT.Copy, scale=0.5).then_inc(s_init, 1)
            act.wait_ge(s_init, 4)
            act.sem_inc(s_sq, 2)
            act.sem_inc(s_exp, 2)
            act.sem_inc(s_mrow, 48)
            for tk in PRE:
                task("pre", 0, tk)
            with act.Fori(0, NB // E) as group, act.Fori(0, E) as e:
                i = group * E + e
                for n in range(0, STEPS, 2):
                    exp_t(i, n)
                    squares(i, n)
                    for tk in STEP[n]:
                        task("body", i, tk)
                    squares(i, n + 1)
                    exp_t(i, n + 1)
                    for tk in STEP[n + 1]:
                        task("body", i, tk)
            task("tail", NB, TAIL[0])
            for n in range(LAG_T):
                exp_t(NB, n)
            for tk in TAIL[1:]:
                task("tail", NB, tk)

        @block.vector
        def _(dve):
            pos = {"n": 0, "base": 0}

            def chain(i, ins):
                pos["n"] += 1
                ins.then_inc(s_dchain, 1)
                dve.wait_ge(s_dchain, i * pos["per"] + pos["base"] + pos["n"] if pos["loop"] else pos["base"] + pos["n"])

            def row_max(i, n):
                r, t = n // T % RING, n % T
                if t == 0:
                    dve.wait_ge(s_stat, i * U + n // T + 1)
                dve.wait_ge(s_scores, i * STEPS + n + 1)
                nc.vector.tensor_reduce(negmax[:, r, t:t + 1], ps_s[:, n % 2, :], axis=AX, op=ALU.max, negate=True)\
                    .then_inc(s_max, 1)

            def row_min(i, n):
                r, t = n // T % RING, n % T
                dve.wait_ge(s_sq, i * STEPS + n + 3)
                nc.vector.tensor_reduce(rowmin[:, r, t:t + 1], ps_s[:, n % 2, :], axis=AX, op=ALU.min)\
                    .then_inc(s_min, 1)

            def divide(i, n):
                j = n // T
                u = (j - 2) % U
                dve.wait_ge(s_pv, i * STEPS + n + 3)
                if j == 2:
                    wait_side(dve, "body", i, "pool", ("snap",))
                o = ps_o[:, 0:T * VW].rearrange("p (t c) -> p t c", t=T)
                chain(i, nc.vector.reciprocal(recip[:, u, :], o[:, :, HD]))
                nc.vector.tensor_tensor(mean_all[:, u, :], o[:, :, HD], recip[:, u, :], ALU.mult)
                nc.vector.tensor_tensor(o_all[:, u, :, :], o[:, :, 0:HD],
                                        recip[:, u, :].unsqueeze(2).to_broadcast([P, T, HD]), ALU.mult)\
                    .then_inc(s_o, 1)

            def moments(i, src, k):
                for t in range(T):
                    last = nc.vector.bn_stats(bn[:, t, :], src[:, t, :])
                chain(i, last)
                dve.nop(nofuse=True)
                for t in range(T):
                    last = nc.vector.bn_aggr(mv[:, k, t, :], bn[:, t, :])
                return last

            def task(phase, i, tk):
                kind = tk[0]
                if "dve" not in ENGINES[kind]:
                    return
                w = lambda of, t: wait_side(dve, phase, i, of, t)
                if "pe" in ENGINES[kind]:
                    w("pe", tk)
                four = ps_w[:, :].rearrange("p (q c) -> p q c", q=4)
                if kind == "win":
                    last = nc.vector.tensor_copy(winm[:, :], ps_w[0:H * 8, 0:T * NW])
                elif kind == "hid1":
                    last = nc.vector.tensor_scalar(hid1[:, :, :].rearrange("p g w -> p (g w)"), ps_w[:, :],
                                                   g1b[:, :], 0.0, ALU.add, ALU.max)
                elif kind == "hid2":
                    last = nc.vector.tensor_scalar(hid2[:, :, :].rearrange("p g w -> p (g w)"), ps_w[0:4 * HD, :],
                                                   g2b[:, :], 0.0, ALU.add, ALU.max)
                elif kind == "alpha":
                    last = nc.vector.tensor_copy(alpha_q[:, :], ps_w[:, 0:T * H])
                elif kind == "wo":
                    k = 4 * tk[1]
                    if k == 0:
                        w("pool", None)
                    last = nc.vector.tensor_tensor(h2[:, k:k + 4, :], four, h_cur[:, k:k + 4, :], ALU.add)
                elif kind == "ln2":
                    w("dve", ("wo", 1))
                    last = moments(i, h2, 0)
                elif kind == "ln3":
                    w("pool", ("ln2",))
                    last = moments(i, x2, 1)
                elif kind == "next":
                    k = 4 * tk[1]
                    if k == 0:
                        dve.wait_ge(s_out, i * 16 + 16)
                    last = nc.vector.tensor_tensor(z[:, k:k + 4, :], four,
                                                   row[:, 1, :].unsqueeze(1).to_broadcast([P, 4, P]), ALU.add)
                elif kind == "h2e":
                    k = 4 * tk[1]
                    if k == 0 and phase == "body":
                        w("pool", ("hcopy",))
                    last = nc.vector.tensor_tensor(h_next[:, k:k + 4, :], four,
                                                   row[:, 0, :].unsqueeze(1).to_broadcast([P, 4, P]), ALU.add)
                elif kind == "ln1":
                    w("dve", ("h2e", 1))
                    last = moments(i, h_next, 2)
                elif kind == "v":
                    k = 4 * tk[1]
                    if k == 0 and phase == "body":
                        w("pool", ("vcopy", 1))
                    for q in range(4):
                        last = nc.vector.tensor_copy(
                            v_next[:, k + q, :].rearrange("p (h c) -> p h c", h=H)[:, :, 0:HD],
                            four[:, q, :].rearrange("p (h c) -> p h c", h=H))
                last.then_inc(side_sem["dve"], 1)

            for t in (g1, g2, g3):
                last = nc.vector.memset(t[:].rearrange("p a b -> p (a b)") if len(t.shape) == 3 else t[:, :], 0.0)
            last.then_inc(s_init, 1)
            for t in (negmax, rowmin, sumsq):
                nc.vector.memset(t[:, :, :], 0.0)
            for t in (recip, mean_all, sq_all, dif_all):
                nc.vector.memset(t[:, :, :], 0.0)
            nc.vector.memset(exps[:, :, :], 1.0)
            nc.vector.memset(qst[:, :, :], 0.0)
            nc.vector.memset(kst[:, :, :], 0.0)
            nc.vector.memset(half_pow[:, :], 0.5)
            nc.vector.memset(rs_pow[:, :], -0.5)
            nc.vector.memset(xc[:, :, 0:1], 0.0)
            last = nc.vector.memset(xc[:, :, L + 1:L + 2], 0.0)
            pos.update(loop=False, base=0, per=0)
            chain(0, last)
            last = nc.vector.memset(kst[KSC:KST, :, :], 1.0)
            last.then_inc(s_init, 1)
            dve.sem_inc(s_min, 2)
            dve.sem_inc(s_out, 16)
            dve.wait_ge(s_load, 16 * N_LOADS)
            dve.wait_ge(s_init, 4)
            for tk in PRE:
                task("pre", 0, tk)
            pos.update(loop=True, base=pos["n"], n=0, per=U + 3)
            with dve.Fori(0, NB // E) as group, dve.Fori(0, E) as e:
                i = group * E + e
                for n in range(0, STEPS, 2):
                    row_max(i, n)
                    row_max(i, n + 1)
                    for k in (n, n + 1):
                        for tk in STEP[k]:
                            task("body", i, tk)
                        row_min(i, k)
                    if (n + 1) % T == LAG_V % T - 1:
                        divide(i, n + 1)
            assert pos["n"] == pos["per"], pos
            pos.update(n=0)
            for n in range(LAG_V):
                if n % T == LAG_V % T - 1:
                    divide(NB, n)
            for tk in TAIL:
                task("tail", NB, tk)

        @block.gpsimd
        def _(pool):
            pos = {"n": 0, "base": 0, "loop": False, "per": 0}

            def chain(i, ins):
                pos["n"] += 1
                ins.then_inc(s_pchain, 1)
                pool.wait_ge(s_pchain, i * pos["per"] + pos["base"] + pos["n"] if pos["loop"]
                             else pos["base"] + pos["n"])

            tt = nc.gpsimd.tensor_tensor

            def ts(*args):
                pool.nop(nofuse=True)
                return nc.gpsimd.tensor_scalar(*args)

            def copy(dst, src):
                return ts(dst, src, 1.0, 1.0, ALU.mult, ALU.mult)

            def statistics(i, n):
                j = n // T
                u = (j - 2) % U
                r = u % RING
                pool.wait_ge(s_o, i * U + j + 1)
                pool.wait_ge(s_sq, i * STEPS + max(T * (j - 2) + T + 2, 2))
                if j == 2:
                    wait_side(pool, "body", i, "act", ("snap",))
                    wait_side(pool, "body", i, "pool", ("snap",))
                tt(dif_all[:, u, :], rowmin[:, r, :], negmax[:, r, :], ALU.add)
                chain(i, tt(sq_all[:, u, :], sumsq[:, r, :], recip[:, u, :], ALU.mult))
                tt(sq_all[:, u, :], sq_all[:, u, :], recip[:, u, :], ALU.mult).then_inc(s_stat, 1)

            def normalise(i, dst, src, k):
                chain(i, ts(rstd[:, k, :], mv[:, k, :, 1], 1.0, EPS, ALU.mult, ALU.add))
                chain(i, tt(rstd[:, k, :], rstd[:, k, :], rs_pow[:, :], ALU.pow))
                chain(i, tt(dst[:, :, :], src[:, :, :], mv[:, k, :, 0].unsqueeze(2).to_broadcast([P, T, P]),
                            ALU.subtract))
                return tt(dst[:, :, :], dst[:, :, :], rstd[:, k, :].unsqueeze(2).to_broadcast([P, T, P]), ALU.mult)

            def task(phase, i, tk):
                kind = tk[0]
                w = lambda of, t: wait_side(pool, phase, i, of, t)
                if kind == "gather":
                    b = 0 if phase == "pre" else i + 1
                    pool.wait_ge(s_idx, 16 if phase == "pre" else i * 16 + 32)
                    w("pe", None)
                    pool.nop(nofuse=True)
                    for t in range(T):
                        nc.gpsimd.indirect_dma_start(out=emb[:, t, :], out_offset=None, in_=table[:, :],
                                                     in_offset=bass.IndirectOffsetOnAxis(ap=idx[:, t:t + 1], axis=0))\
                            .then_inc(s_emb, 16)
                    return
                if "pool" not in ENGINES[kind]:
                    return
                wait_own(pool, phase, i, "pool", tk)
                if kind == "mrow":
                    j = tk[1]
                    r = (j - 1) % RING
                    if j:
                        pool.wait_ge(s_max, i * STEPS + T * j)
                    else:
                        pool.wait_ge(s_min, i * STEPS + 2)
                    if j == 0:
                        w("pe", None)
                    else:
                        w("pe", ("mrow", j - 1))
                    chain(i, copy(mparts[:, 0, :], negmax[:, r, :]))
                    chain(i, tt(mrest[:, 0, :], negmax[:, r, :], mparts[:, 0, :], ALU.subtract))
                    chain(i, copy(mparts[:, 1, :], mrest[:, 0, :]))
                    last = tt(mparts[:, 2, :], mrest[:, 0, :], mparts[:, 1, :], ALU.subtract)
                elif kind == "vcopy":
                    if tk[1] == 0:
                        w("dve", None)
                        pool.wait_ge(s_pv, i * STEPS + 2)
                        last = copy(v_cur[:, :, 0:6 * VW], v_next[:, :, 0:6 * VW])
                    else:
                        pool.wait_ge(s_pv, i * STEPS + LAG_V - 1 + 3)
                        last = copy(v_cur[:, :, 6 * VW:], v_next[:, :, 6 * VW:])
                elif kind == "hcopy":
                    w("dve", ("wo", 1))
                    last = copy(h_cur[:, :, :], h_next[:, :, :])
                elif kind == "snap":
                    pool.wait_ge(s_stat, i * U + 3)
                    if phase == "body":
                        w("pe", None)
                    oa = o_all[:, :, :, :].rearrange("p u t d -> p t u d")
                    heads = lambda t: t[:, :, :].rearrange("p t (h d) -> p t h d", h=H)
                    tt(heads(odif), oa[:, :, 0:H, :], oa[:, :, H:U, :], ALU.subtract)
                    copy(heads(o2), oa[:, :, H:U, :])
                    flat = lambda t: t[:, :, :].rearrange("p u t -> p (u t)")

                    def feature(f, fn):
                        for a in range(2):
                            last = fn(gin[:, :, :, 4 * a + f].rearrange("p t h -> p h t"), a)
                        return last

                    def of(src, a):
                        return src[:, H * a:H * a + H, :]

                    def of2(k, a):
                        return gtmp[:, k, U * T // 2 * a:U * T // 2 * (a + 1)].rearrange("p (h t) -> p h t", h=H)
                    feature(0, lambda dst, a: ts(dst, of(mean_all, a), 1.0 / L, 1.0, ALU.mult, ALU.mult))
                    feature(2, lambda dst, a: copy(dst, of(recip, a)))
                    chain(i, tt(gtmp[:, 1, :], flat(mean_all), flat(mean_all), ALU.mult))
                    chain(i, ts(gtmp[:, 2, :], gtmp[:, 1, :], 1.0 / L, 1.0, ALU.mult, ALU.mult))
                    chain(i, tt(gtmp[:, 1, :], flat(sq_all), gtmp[:, 2, :], ALU.subtract))
                    chain(i, ts(gtmp[:, 3, :], gtmp[:, 1, :], 1.0 / (L - 1), 0.0, ALU.mult, ALU.max))
                    feature(1, lambda dst, a: tt(dst, of2(3, a),
                                                 half_pow[:, :].rearrange("p (h t) -> p h t", h=H), ALU.pow))
                    w("act", tk)
                    last = feature(3, lambda dst, a: tt(dst, of2(0, a), of(recip, a), ALU.mult))
                elif kind == "logit":
                    w("act", tk)
                    last = ts(alpha_w[:, 1, :], alpha_w[:, 0, :], 0.5, 0.5, ALU.mult, ALU.add)
                elif kind == "alpha":
                    w("dve", tk)
                    flat = lambda t: t[:, :, :].rearrange("p t (h d) -> p (t h) d", h=H)
                    chain(i, tt(flat(att), flat(odif), alpha_q[:, :].unsqueeze(2).to_broadcast([P, T * H, HD]),
                                ALU.mult))
                    last = tt(flat(att), flat(att), flat(o2), ALU.add)
                elif kind == "ln2":
                    w("dve", tk)
                    last = normalise(i, x2, h2, 0)
                elif kind == "ln3":
                    w("dve", tk)
                    w("pe", ("attT", 1))
                    chain(i, normalise(i, att, x2, 1))
                    chain(i, tt(att[:, :, :], att[:, :, :], row[:, 2, :].unsqueeze(1).to_broadcast([P, T, P]),
                                ALU.mult))
                    last = tt(att[:, :, :], att[:, :, :], row[:, 3, :].unsqueeze(1).to_broadcast([P, T, P]), ALU.add)
                elif kind == "gelu2":
                    w("act", tk)
                    last = tt(z[:, :, :], z[:, :, :], h2[:, :, :], ALU.add)
                elif kind == "convg":
                    _, l, c = tk
                    w("act", tk)
                    x_in = xc[:, l % 2, 1 + CH * c:1 + CH * c + CH]
                    x_out = xc[:, (l + 1) % 2, 1 + CH * c:1 + CH * c + CH]
                    ts(ctmp[:, 3, :], x_in, RES, 1.0, ALU.mult, ALU.mult)
                    chain(i, tt(ctmp[:, 0, :], ug[:, c % 2, :], va[:, c % 2, :], ALU.mult))
                    chain(i, tt(ctmp[:, 1, :], ctmp[:, 0, :], va[:, c % 2, :], ALU.add))
                    chain(i, ts(ctmp[:, 2, :], ctmp[:, 1, :], 0.5, RES, ALU.mult, ALU.mult))
                    last = tt(x_out, ctmp[:, 2, :], ctmp[:, 3, :], ALU.add)
                elif kind == "ln1":
                    w("dve", tk)
                    last = normalise(i, xn, h_next, 2)
                elif kind == "qk":
                    _, a, which, k = tk
                    w("act", tk)
                    dst = part[:, a, which, :, 512 * k:512 * k + 512]
                    chain(i, copy(dst[:, 0, :], stage[:, k, :]))
                    chain(i, tt(srest[:, :], stage[:, k, :], dst[:, 0, :], ALU.subtract))
                    chain(i, copy(dst[:, 1, :], srest[:, :]))
                    last = tt(dst[:, 2, :], srest[:, :], dst[:, 1, :], ALU.subtract)
                last.then_inc(side_sem["pool"], 1)

            for t in (v_next, v_cur, h_cur, ):
                nc.gpsimd.memset(t[:, :, :], 0.0)
            last = nc.gpsimd.memset(o_all[:, :, :, :], 0.0)
            chain(0, last)
            for t in (v_next, v_cur):
                last = nc.gpsimd.memset(t[:, :, :].rearrange("p t (h c) -> p (t h) c", c=VW)[:, :, HD:VW], 1.0)
            pool.wait_ge(s_load, 16 * N_LOADS)
            nc.gpsimd.tensor_scalar(ident_b[:, :], ident, 1.0, 1.0, ALU.mult, ALU.mult).then_inc(s_init, 1)
            pool.sem_inc(s_pv, 2)
            pool.sem_inc(s_stat, 1)
            pool.wait_ge(s_init, 4)
            for tk in PRE:
                task("pre", 0, tk)
            per = 0
            for tk in BODY:
                per += {"mrow": 3, "snap": 4, "alpha": 1, "ln2": 3, "ln3": 5, "convg": 3, "ln1": 3, "qk": 3}.get(tk[0], 0)
            pos.update(loop=True, base=pos["n"], n=0, per=per + U)
            with pool.Fori(0, NB // E) as group, pool.Fori(0, E) as e:
                i = group * E + e
                for n in range(STEPS):
                    for tk in STEP[n]:
                        task("body", i, tk)
                    if n % T == LAG_V % T - 1:
                        statistics(i, n)
            assert pos["n"] == pos["per"], pos
            pos.update(n=0)
            task("tail", NB, TAIL[0])
            for n in range(LAG_V):
                if n % T == LAG_V % T - 1:
                    statistics(NB, n)
            for tk in TAIL[1:]:
                task("tail", NB, tk)


def _constants():
    c = np.zeros((P, P + NW + P), np.float32)
    c[:, 0:P] = np.eye(P)
    for q in range(P):
        c[q, P + q // WS] = 1.0 / WS
        c[q // WS, P + NW + q] = 1.0
    return c


def kernel(**inputs):
    import concourse.bacc as _bacc
    from concourse.bass_utils import run_bass_kernel_spmd as _run

    a = {k: np.asarray(v) for k, v in inputs.items()}
    nb = a["x"].shape[0]
    ids = np.zeros((nb + 1, P, T), np.int32)
    ids[:nb] = a["x"].reshape(nb, T, P).transpose(0, 2, 1)
    f = {k[3:]: v for k, v in a.items() if k.startswith("L0_")}
    before = [(e - 1) % E for e in range(E)]
    arrays = {
        "ids": ids, "table": f["tok_emb_table"], "consts": _constants(),
        "w_e2h": f["tok_W_e2h"], "b_e2h": f["tok_b_e2h"].reshape(P, 1),
        "conv_w": f["tok_conv_w"].transpose(2, 0, 3, 1),
        "conv_b": f["tok_conv_b"].reshape(2 * LAYERS, P).T,
        "w_h2e": f["tok_W_h2e"], "b_h2e": f["tok_b_h2e"].reshape(1, P),
        "wq1": f["attn_Wq1"], "wk1": f["attn_Wk1"], "wq2": f["attn_Wq2"], "wk2": f["attn_Wk2"],
        "wv": f["attn_Wv"], "wo": f["attn_Wo"],
        "gw1": f["attn_gw1"], "gb1": f["attn_gb1"].reshape(-1, 1), "gw2": f["attn_gw2"],
        "gb2": f["attn_gb2"].reshape(-1, 1), "gw3": f["attn_gw3"], "gb3": f["attn_gb3"].reshape(1, 1),
        "ln_g": f["ffn_ln_g"].reshape(1, P), "ln_b": f["ffn_ln_b"].reshape(1, P),
        "attn_w": f["ffn_attn_w"].T, "attn_b": f["ffn_attn_b"].reshape(P, 1),
        "fc1_w": f["ffn_fc1_w"].transpose(0, 2, 1)[before],
        "fc1_b": f["ffn_fc1_b"].reshape(E, FC, P).transpose(0, 2, 1)[before],
        "fc2_w": f["ffn_fc2_w"].reshape(E, P, FC, P).transpose(0, 3, 2, 1)[before],
        "fc2_b": f["ffn_fc2_b"].reshape(E, P, 1)[before],
        "next_w": f["ffn_next_w"].T, "next_b": f["ffn_next_b"].reshape(1, P),
    }
    nc = _bacc.Bacc("TRN2", target_bir_lowering=False, num_devices=1)
    feed, args = {}, {}
    for name, v in arrays.items():
        v = np.ascontiguousarray(v)
        feed[f"in_{name}"] = v
        args[name] = nc.dram_tensor(f"in_{name}", v.shape, mybir.dt.from_np(v.dtype), kind="ExternalInput").ap()
    store = nc.dram_tensor("out_dram", (nb + 1, T, P, P), F32, kind="ExternalOutput").ap()
    tower_kernel(nc, out=store.rearrange("b t p d -> b p t d"), **args)
    r = _run(nc, [feed], core_ids=[0])
    return np.asarray(r.results[0]["out_dram"])[1:].reshape(nb, L, P)
```

```python
from contextlib import ExitStack

import numpy as np

import concourse.bass as bass
from concourse import mybir

F32 = mybir.dt.float32
BF16 = mybir.dt.bfloat16
I32 = mybir.dt.int32
ALU = mybir.AluOpType
ACT = mybir.ActivationFunctionType
AX = mybir.AxisListType.X

P = 128
L = 1024
T = L // P
H = 8
HD = P // H
VW = HD + 1
U = 2 * H
STEPS = U * T
E = 8
FC = 4
WS = 4
NW = P // WS
LAYERS, TAPS = 6, 3
RING = 4
NPART = 6
KSC = NPART * HD
KST = KSC + 3
Q_PART = (0, 0, 0, 1, 1, 2)
K_PART = (0, 1, 2, 0, 1, 0)
LAG_T = T + 4
LAG_V = LAG_T + 2
CH = 256
NC = L // CH
RES = 0.7071067811865476
EPS = 1e-5
QC = L // 4

def two(kind):
    return [(kind, 0), (kind, 1)]


CONV = [("conv" + half, l, c) for l in range(LAYERS) for c in range(NC) for half in "ag"]
QK = [[("qk", a, w, k) for w in range(2) for k in range(2)] for a in range(2)]
PRE = [("gather",)] + two("embT") + two("e2h") + CONV + two("h2e") + [("ln1",)] + two("xnT") + QK[0] + two("v")
POST = ([("snap",), ("std",), ("win",), ("hid1",), ("hid2",), ("logit",), ("alpha",)] + two("attT") + two("wo")
        + [("ln2",), ("ln3",)] + two("nT") + [("attw", c) for c in range(NC)]
        + [("fc1", c, j) for c in range(NC) for j in range(2)] + [("gelu1",)]
        + [("fc2", c) for c in range(NC)] + two("next") + [("gelu2",)])
ENGINES = {
    "msplit": ("pool",), "mrow": ("pe", "act"), "unit": ("pe", "dve", "pool"), "vcopy": ("pool",), "hcopy": ("pool",), "snap": ("pool", "act"),
    "std": ("act",),
    "win": ("pe", "dve"), "hid1": ("pe", "dve"), "hid2": ("pe", "dve"), "logit": ("pe", "act", "pool"),
    "alpha": ("pe", "dve", "pool"), "attT": ("pe", "act"), "wo": ("pe", "dve"), "ln2": ("dve", "pool"),
    "ln3": ("dve", "pool"), "nT": ("pe", "act"), "attw": ("pe", "act"), "fc1": ("pe", "act"), "gelu1": ("act",),
    "fc2": ("pe", "act"), "next": ("pe", "dve"), "gelu2": ("act", "pool"), "gather": (), "embT": ("pe", "act"),
    "e2h": ("pe", "act"), "conva": ("pe", "act"), "convg": ("pe", "act", "pool"), "h2e": ("pe", "dve"),
    "ln1": ("dve", "pool"), "xnT": ("pe", "act"), "qk": ("pe", "act", "pool"), "v": ("pe", "dve"),
}
READER = {k: ("dve" if "dve" in v else "act") for k, v in ENGINES.items() if "pe" in v}


COST = {"mrow": 1, "unit": 4, "win": 5, "hid1": 9, "hid2": 9, "logit": 8, "alpha": 3, "attT": 4, "wo": 9, "nT": 4,
        "attw": 7, "fc1": 9, "fc2": 18, "next": 9, "embT": 4, "e2h": 9, "conva": 13, "convg": 13, "h2e": 9, "xnT": 4,
        "qk": 9, "v": 9}
GAP = {("std",): 2, ("win",): 2, ("hid1",): 2, ("hid2",): 2, ("logit",): 2, ("alpha",): 2, ("attT", 0): 3,
       ("wo", 0): 2, ("ln3",): 5, ("nT", 0): 6, ("attw", 0): 2, ("gelu1",): 1, ("fc2", 0): 4, ("next", 0): 2,
       ("embT", 0): 1, ("e2h", 0): 2, ("conva", 0, 0): 2, ("h2e", 1): 3, ("ln1",): 2, ("xnT", 0): 5,
       **{task: 2 for task in QK[0]}}


SLOTS = {"ln1": (2, 3, 4), "ln2": (0, 1, 2, 3, 4), "ln3": (0, 1, 2, 3), "alpha": (0, 1, 2, 3, 4),
         "gelu2": (0, 1, 2, 3, 4), "snap": (0, 1)}


def plan():
    at = {n: [] for n in range(STEPS)}
    for j in range(U):
        at[j * T].append(("mrow", j))
        at[j * T + LAG_V % T + 1].append(("unit", j))
    for n, task in {1: QK[1][0], 3: QK[1][1], 4: ("vcopy", 0), 5: QK[1][2], 9: QK[1][3], 10: ("gather",),
                    14: ("vcopy", 1)}.items():
        at[n].append(task)
    post, pre = [list(POST), T + LAG_V % T + 2], [list(PRE[1:]), T + 6]
    cost = lambda tasks: sum(COST.get(t[0], 0) for t in tasks)
    share = cost(BODY_TASKS) / (STEPS - 2 * T)
    for n in range(STEPS):
        for stage in (post, pre):
            tasks, first = stage
            while tasks and first <= n and n % T in SLOTS.get(tasks[0][0], range(T)):
                task = tasks[0]
                done = cost([t for m in range(n) for t in at[m]])
                on_pe = task[0] in COST
                if stage is pre and on_pe and at[n] and cost(at[n]) + COST[task[0]] > 18:
                    break
                if stage is pre and on_pe and done + cost(at[n]) + COST[task[0]] / 2 > share * (n + 1):
                    break
                at[n].append(tasks.pop(0))
                if task == ("wo", 1):
                    at[n].append(("hcopy",))
                first = n + (GAP.get(tasks[0], 1) if tasks else 0)
            stage[1] = first
    assert not post[0] and not pre[0], (post, pre)
    for j in range(1, U + 1):
        at[j * T - 2].append(("msplit", j))
    return at


BODY_TASKS = [("mrow", j) for j in range(U)] + [("unit", j) for j in range(U)] + QK[1] + POST + PRE
STEP = plan()
BODY = [task for n in range(STEPS) for task in STEP[n]]
TAIL = [("mrow", 0), ("unit", 0), ("unit", 1)] + POST
PHASES = {"pre": PRE, "body": BODY, "tail": TAIL}


class Side:

    def __init__(self, sems):
        self.sems = sems

    def upto(self, phase, i, eng, task):
        tasks = PHASES[phase]
        n = 0 if task is None else tasks.index(task) + 1
        count = sum(eng in ENGINES[t[0]] for t in tasks[:n])
        if phase == "pre":
            return count
        count += sum(eng in ENGINES[t[0]] for t in PRE)
        return i * sum(eng in ENGINES[t[0]] for t in BODY) + count


def tower_kernel(nc, ids, table, consts, w_e2h, b_e2h, conv_w, conv_b, w_h2e, b_h2e, wq1, wk1, wq2, wk2, wv, wo,
                 gw1, gb1, gw2, gb2, gw3, gb3, ln_g, ln_b, attn_w, attn_b, fc1_w, fc1_b, fc2_w, fc2_b,
                 next_w, next_b, out):
    NB = ids.shape[0] - 1

    with ExitStack() as ctx:
        def sb(name, shape, dt=F32):
            return ctx.enter_context(nc.sbuf_tensor(name, shape, dt))

        def sem(name):
            return ctx.enter_context(nc.semaphore(name))

        ps_s = ctx.enter_context(nc.psum_tensor("ps_s", [P, 2, L], F32))
        ps_t = ctx.enter_context(nc.psum_tensor("ps_t", [P, 2, 512], F32))
        ps_o = ctx.enter_context(nc.psum_tensor("ps_o", [P, 512], F32))
        ps_w = ctx.enter_context(nc.psum_tensor("ps_w", [P, 512], F32))

        cst = sb("cst", [P, P + NW + P])
        ident = cst[:, 0:P]
        win_mean = cst[:, P:P + NW]
        win_rep = cst[0:NW, P + NW:P + NW + P]
        ident_b = sb("ident_b", [P, P], BF16)
        cw = sb("cw", [P, LAYERS, TAPS, 2 * P])
        cb = sb("cb", [P, 2 * LAYERS])
        cb_half = sb("cb_half", [P, 2 * LAYERS])
        we2h, wh2e = sb("we2h", [P, P]), sb("wh2e", [P, P])
        wqk = sb("wqk", [P, 2, 2, P])
        wv_s, wo_s, wattn, wnext = sb("wv_s", [P, P]), sb("wo_s", [P, P]), sb("wattn", [P, P]), sb("wnext", [P, P])
        col = sb("col", [P, 2])
        row = sb("row", [P, 4, P])
        g1 = sb("g1", [H * 8, 2, P])
        g2 = sb("g2", [P, 4 * HD])
        g3 = sb("g3", [4 * HD, 4])
        g1b, g2b = sb("g1b", [P, 1]), sb("g2b", [4 * HD, 1])
        g3b, g3h = sb("g3b", [NW, 1]), sb("g3h", [NW, 1])
        rs_pow = sb("rs_pow", [P, T])

        part = sb("part", [P, 2, 2, 3, L], BF16)
        qst = sb("qst", [KST, RING, L], BF16)
        kst = sb("kst", [KST, RING, L], BF16)
        exps = sb("exps", [P, RING, L])
        junk = sb("junk", [P, 2, L], BF16)
        negmax, rowmin, sumsq = (sb(n, [P, RING, T]) for n in ("negmax", "rowmin", "sumsq"))
        mparts = sb("mparts", [P, 3, T], BF16)
        mrest = sb("mrest", [P, 2, T])
        mrow = sb("mrow", [3 * T, P], BF16)
        v_next, v_cur = sb("v_next", [P, T, H * VW]), sb("v_cur", [P, T, H * VW + 32 - VW])
        o_t = sb("o_t", [P, QC])
        o_all = sb("o_all", [P, U, T, HD])
        recip, mean_all, sq_all, dif_all = (sb(n, [P, U, T]) for n in ("recip", "mean_all", "sq_all", "dif_all"))

        gin = sb("gin", [P, T, H, 8])
        gtmp = sb("gtmp", [P, 4, U * T])
        winm = sb("winm", [H * 8, T * NW])
        hid1 = sb("hid1", [P, 2, T * NW])
        hid2 = sb("hid2", [4 * HD, 2, T * NW])
        alpha_w = sb("alpha_w", [NW, 2, T * H])
        alpha_q = sb("alpha_q", [P, T * H])
        odif, o2 = sb("odif", [P, T, P]), sb("o2", [P, T, P])
        att = sb("att", [P, T, P])
        chan = sb("chan", [P, L])
        h_next, h_cur, h2 = sb("h_next", [P, T, P]), sb("h_cur", [P, T, P]), sb("h2", [P, T, P])
        x2 = sb("x2", [P, T, P])
        bn = sb("bn", [P, T, 6])
        mv = sb("mv", [P, 3, T, 2])
        rstd = sb("rstd", [P, 3, T])
        xa = sb("xa", [P, L])
        hpre = sb("hpre", [P, FC, L])
        y = chan
        z = sb("z", [P, T, P])
        fc1s, fc2s = sb("fc1s", [P, FC * P]), sb("fc2s", [P, FC, P])
        fc1bs, fc2bs = sb("fc1bs", [P, FC]), sb("fc2bs", [P, 1])

        idx = sb("idx", [P, T], I32)
        xc = sb("xc", [P, 2, L + 2])
        va, ug = sb("va", [P, 2, CH]), sb("ug", [P, 2, CH])
        ctmp = sb("ctmp", [P, 4, CH])
        xn = sb("xn", [P, T, P])
        xn_t = sb("xn_t", [P, L])
        emb, emb_t = xn, xn_t
        stage = sb("stage", [P, 2, 512])
        srest = ctmp[:, 0:2, :].rearrange("p a b -> p (a b)")

        s_load = sem("s_load")
        s_init = sem("s_init")
        s_scores = sem("s_scores")
        s_max = sem("s_max")
        s_min = sem("s_min")
        s_sq = sem("s_sq")
        s_st = sem("s_st")
        s_exp = sem("s_exp")
        s_pv = sem("s_pv")
        s_ot = sem("s_ot")
        s_ring = [sem(f"s_ring{r}") for r in range(RING)]
        s_mrow = sem("s_mrow")
        s_idx = sem("s_idx")
        s_emb = sem("s_emb")
        s_exw = sem("s_exw")
        s_out = sem("s_out")
        s_dchain = sem("s_dchain")
        s_pchain = sem("s_pchain")
        side_sem = {e: sem("side_" + e) for e in ("pe", "act", "dve", "pool")}
        side = Side(side_sem)

        def wait_side(eng, phase, i, of, task=None):
            eng.wait_ge(side_sem[of], side.upto(phase, i, of, task))

        def wait_bank(eng, phase, i, task):
            tasks = PHASES[phase]
            before = [t for t in tasks[:tasks.index(task)] if t[0] in READER]
            if before:
                wait_side(eng, phase, i, READER[before[-1][0]], before[-1])
            elif phase == "body":
                wait_side(eng, phase, i, "act")
                wait_side(eng, phase, i, "dve")
            elif phase == "tail":
                wait_side(eng, phase, i, "act")
                wait_side(eng, phase, i, "dve")

        def wait_own(eng, phase, i, name, task):
            tasks = PHASES[phase]
            before = [t for t in tasks[:tasks.index(task)] if name in ENGINES[t[0]]]
            if before or phase != "pre":
                wait_side(eng, phase, i, name, before[-1] if before else None)

        def setup_loads(eng):
            n = 0
            pairs = [(cst[:, :], consts), (cw[:, :, :, :], conv_w), (cb[:, :], conv_b), (we2h[:, :], w_e2h),
                     (wh2e[:, :], w_h2e), (wqk[:, 0, 0, :], wq1), (wqk[:, 0, 1, :], wk1), (wqk[:, 1, 0, :], wq2),
                     (wqk[:, 1, 1, :], wk2), (wv_s[:, :], wv), (wo_s[:, :], wo), (wattn[:, :], attn_w),
                     (wnext[:, :], next_w), (col[:, 0:1], b_e2h), (col[:, 1:2], attn_b)]
            for k, b in enumerate((b_h2e, next_b, ln_g, ln_b)):
                pairs.append((row[:, k, :], b.to_broadcast([P, P])))
            for h in range(H):
                pairs.append((g1[8 * h:8 * h + 8, h // 4, 32 * (h % 4):32 * (h % 4) + 32], gw1))
            for j in range(4):
                pairs.append((g2[32 * j:32 * j + 32, HD * j:HD * j + HD], gw2))
                pairs.append((g3[HD * j:HD * j + HD, j:j + 1], gw3))
                pairs.append((g1b[32 * j:32 * j + 32, :], gb1))
                pairs.append((g2b[HD * j:HD * j + HD, :], gb2))
            pairs.append((g3b[:, :], gb3.to_broadcast([NW, 1])))
            for dst, src in pairs:
                eng.dma_start(dst, src).then_inc(s_load, 16)
                n += 1
            return n

        N_LOADS = 15 + 4 + H + 16 + 1

        block = ctx.enter_context(nc.Block())

        @block.sync
        def _(sp):
            def settle():
                sp.nop(nofuse=True)

            sp.wait_ge(s_init, 1)
            assert setup_loads(sp) == N_LOADS

            def load_ids(b):
                sp.dma_start(idx[:, :], ids[b]).then_inc(s_idx, 16)

            def load_unit(u):
                a, h, r = u // H, u % H, u % RING
                for g in range(NPART):
                    for dst, w, c in ((qst, 0, Q_PART[g]), (kst, 1, K_PART[g])):
                        sp.dma_start(dst[HD * g:HD * g + HD, r, :], part[HD * h:HD * h + HD, a, w, c, :])\
                          .then_inc(s_ring[r], 16)

            def store_mrow(phase, i, j):
                wait_side(sp, phase, i, "act", ("mrow", j))
                settle()
                for c in range(3):
                    sp.dma_start(qst[KSC + c:KSC + c + 1, (j - 1) % RING, :].rearrange("o (t q) -> o t q", t=T),
                                 mrow[T * c:T * c + T, :]).then_inc(s_mrow, 16)

            def load_expert(phase, i, e):
                wait_side(sp, phase, i, "pe")
                settle()
                wait_side(sp, phase, i, "act")
                settle()
                for dst, src in ((fc1s[:, :], fc1_w[e]), (fc2s[:, :, :], fc2_w[e]), (fc1bs[:, :], fc1_b[e]),
                                 (fc2bs[:, :], fc2_b[e])):
                    sp.dma_start(dst, src).then_inc(s_exw, 16)

            def store_out(phase, i):
                wait_side(sp, phase, i, "pool", ("gelu2",))
                settle()
                sp.dma_start(out[i], z[:, :, :]).then_inc(s_out, 16)

            load_ids(0)
            wait_side(sp, "pre", 0, "pool", QK[0][-1])
            load_unit(0)
            with sp.Fori(0, NB // E) as group, sp.Fori(0, E) as e:
                i = group * E + e
                sp.wait_ge(s_emb, i * (16 * T) + 16 * T)
                settle()
                load_ids(i + 1)
                load_expert("body", i, e)
                for j in range(U):
                    if j:
                        sp.wait_ge(s_st, i * (2 * STEPS) + 2 * (T * (j - 3) + T - 1 + LAG_T) + 2)
                    else:
                        sp.wait_ge(s_exp, i * (2 * STEPS) + 2)
                    settle()
                    if j + 1 in (U // 2, U):
                        wait_side(sp, "body", i, "pool", QK[(j + 1) % U // H][-1])
                        settle()
                    store_mrow("body", i, j)
                    load_unit((j + 1) % U)
                    if ("gelu2",) in sum((STEP[n] for n in range(j * T, j * T + T)), []):
                        store_out("body", i)
            load_expert("tail", NB, 0)
            store_mrow("tail", NB, 0)
            store_out("tail", NB)
            sp.wait_ge(s_out, 16 * (NB + 2))

        @block.tensor
        def _(pe):
            def mm(dst, lhs, rhs, start=True, stop=True, **kw):
                return nc.tensor.matmul(dst, lhs, rhs, start=start, stop=stop, **kw)

            def scores(i, n):
                u, t = n // T, n % T
                if t == 0:
                    pe.wait_ge(s_ring[u % RING], i * (4 * 12 * 16) + 12 * 16 * (u // RING + 1))
                pe.wait_ge(s_min, i * STEPS + n + 1)
                for c in range(2):
                    last = mm(ps_s[:, n % 2, 512 * c:512 * c + 512], qst[0:KSC, u % RING, P * t:P * t + P],
                              kst[0:KSC, u % RING, 512 * c:512 * c + 512])
                last.then_inc(s_scores, 1)

            def scores_t(i, n):
                m = (n - LAG_T) % STEPS
                u, t = m // T, m % T
                if t == 0:
                    pe.wait_ge(s_mrow, i * (U * 48) + 48 * (n // T + 2))
                for c in range(2):
                    pe.wait_ge(s_exp, i * (2 * STEPS) + 2 * n + c + 1)
                    mm(ps_t[:, c, :], kst[:, u % RING, P * t:P * t + P], qst[:, u % RING, 512 * c:512 * c + 512])\
                        .then_inc(s_st, 1)

            def weighted(i, n, count=True):
                m = (n - LAG_V) % STEPS
                h, t = m // T % H, m % T
                if count:
                    pe.wait_ge(s_exp, i * (2 * STEPS) + max(2 * n, 1))
                    if t == 0:
                        pe.wait_ge(s_ot, i * U + n // T + 1)
                    if m == 0:
                        wait_side(pe, "body", i, "pool", ("vcopy", 0))
                    if m == 6 * T:
                        wait_side(pe, "body", i, "pool", ("vcopy", 1))
                for q in range(4):
                    last = mm(ps_o[32 * q:32 * q + 32, 0:QC], v_cur[:, t, VW * h:VW * h + 32],
                              exps[:, (n - 2) % RING, QC * q:QC * q + QC], start=(t == 0), stop=(t == T - 1))
                if count:
                    last.then_inc(s_pv, 1)

            def turn(src, k):
                for q in range(4):
                    last = nc.tensor.transpose(ps_w[:, P * q:P * q + P], src[:, 4 * k + q, :], ident)
                return last

            def task(phase, i, tk):
                kind = tk[0]
                if "pe" not in ENGINES[kind]:
                    return
                wait_bank(pe, phase, i, tk)
                w = lambda of, t: wait_side(pe, phase, i, of, t)
                if kind == "mrow":
                    w("pool", ("msplit", tk[1]) if tk[1] else None)
                    last = nc.tensor.transpose(ps_w[0:3 * T, 0:P // 2].bitcast(BF16),
                                               mparts[:, :, :].rearrange("p c t -> p (c t)"), ident_b[:, :])
                elif kind == "unit":
                    pe.wait_ge(s_ot, i * U + tk[1] + 1)
                    for q in range(2):
                        last = nc.tensor.transpose(ps_w[:, P * q:P * q + P], o_t[:, P * q:P * q + P], ident)
                elif kind == "win":
                    w("act", ("std",))
                    for t in range(T):
                        last = mm(ps_w[0:H * 8, NW * t:NW * t + NW], gin[:, t, :, :].rearrange("p h f -> p (h f)"),
                                  win_mean)
                elif kind == "hid1":
                    w("dve", ("win",))
                    for g in range(2):
                        last = mm(ps_w[:, CH * g:CH * g + CH], g1[:, g, :], winm[:, :])
                elif kind == "hid2":
                    w("dve", ("hid1",))
                    for g in range(2):
                        last = mm(ps_w[0:4 * HD, CH * g:CH * g + CH], g2[:, :], hid1[:, g, :])
                elif kind == "logit":
                    w("dve", ("hid2",))
                    pe.nop(nofuse=True)
                    for t in range(T):
                        for g in range(2):
                            last = mm(ps_w[0:NW, H * t + 4 * g:H * t + 4 * g + 4],
                                      hid2[:, g, NW * t:NW * t + NW], g3[:, :])
                elif kind == "alpha":
                    w("pool", ("logit",))
                    last = mm(ps_w[:, 0:T * H], win_rep, alpha_w[:, 1, :])
                elif kind == "attT":
                    w("pool", ("alpha",))
                    last = turn(att, tk[1])
                elif kind == "wo":
                    w("act", ("attT", tk[1]))
                    for q in range(4):
                        t = 4 * tk[1] + q
                        last = mm(ps_w[:, P * q:P * q + P], chan[:, P * t:P * t + P], wo_s[:, :])
                elif kind == "nT":
                    w("pool", ("ln3",))
                    last = turn(att, tk[1])
                elif kind == "attw":
                    c = tk[1]
                    w("act", ("nT", c // 2))
                    mm(ps_w[:, 0:CH], wattn[:, :], chan[:, CH * c:CH * c + CH], stop=False, skip_group_check=True)
                    for q in range(2):
                        last = mm(ps_w[:, P * q:P * q + P], x2[:, 2 * c + q, :], ident, start=False,
                                  skip_group_check=True)
                elif kind == "fc1":
                    _, c, j = tk
                    if (c, j) == (0, 0):
                        pe.wait_ge(s_exw, i * 64 + 64)
                    w("act", ("attw", c))
                    for q in range(2):
                        f = 2 * j + q
                        last = mm(ps_w[:, CH * q:CH * q + CH], fc1s[:, P * f:P * f + P], xa[:, CH * c:CH * c + CH])
                elif kind == "fc2":
                    c = tk[1]
                    w("act", ("gelu1",))
                    for f in range(FC):
                        last = mm(ps_w[:, 0:CH], fc2s[:, f, :], hpre[:, f, CH * c:CH * c + CH], start=(f == 0),
                                  stop=(f == FC - 1))
                elif kind == "next":
                    w("act", ("fc2", 2 * tk[1] + 1))
                    for q in range(4):
                        t = 4 * tk[1] + q
                        last = mm(ps_w[:, P * q:P * q + P], y[:, P * t:P * t + P], wnext[:, :])
                elif kind == "embT":
                    pe.wait_ge(s_emb, (16 * T) if phase == "pre" else (i + 2) * (16 * T))
                    last = turn(emb, tk[1])
                elif kind == "e2h":
                    w("act", ("embT", tk[1]))
                    last = mm(ps_w[:, :], we2h[:, :], emb_t[:, 512 * tk[1]:512 * tk[1] + 512])
                elif kind in ("conva", "convg"):
                    _, l, c = tk
                    if l == 0:
                        w("act", ("e2h", min((CH * c + CH) // 512, 1)))
                    else:
                        w("pool", ("convg", l - 1, min(c + 1, NC - 1)))
                    g = kind == "convg"
                    for k in range(TAPS):
                        last = mm(ps_w[:, CH * g:CH * g + CH], cw[:, l, k, P * g:P * g + P],
                                  xc[:, l % 2, CH * c + k:CH * c + k + CH], start=(k == 0), stop=(k == TAPS - 1))
                elif kind == "h2e":
                    w("pool", ("convg", LAYERS - 1, NC // 2 * (tk[1] + 1) - 1))
                    for q in range(4):
                        t = 4 * tk[1] + q
                        last = mm(ps_w[:, P * q:P * q + P], xc[:, 0, 1 + P * t:1 + P * t + P], wh2e[:, :])
                elif kind == "xnT":
                    w("pool", ("ln1",))
                    last = turn(xn, tk[1])
                elif kind == "qk":
                    _, a, which, k = tk
                    if a == 0:
                        w("act", ("xnT", k))
                    last = mm(ps_w[:, :], wqk[:, a, which, :], xn_t[:, 512 * k:512 * k + 512])
                elif kind == "v":
                    w("act", ("xnT", tk[1]))
                    for q in range(4):
                        t = 4 * tk[1] + q
                        last = mm(ps_w[:, P * q:P * q + P], xn_t[:, P * t:P * t + P], wv_s[:, :])
                last.then_inc(side_sem["pe"], 1)

            pe.wait_ge(s_load, 16 * N_LOADS)
            pe.wait_ge(s_init, 3)
            for n in range(-((-LAG_V) % T), 0):
                weighted(0, n, count=False)
            for tk in PRE:
                task("pre", 0, tk)
            with pe.Fori(0, NB // E) as group, pe.Fori(0, E) as e:
                i = group * E + e
                for n in range(0, STEPS, 2):
                    scores(i, n)
                    scores_t(i, n)
                    scores(i, n + 1)
                    for tk in STEP[n]:
                        task("body", i, tk)
                    scores_t(i, n + 1)
                    weighted(i, n)
                    weighted(i, n + 1)
                    for tk in STEP[n + 1]:
                        task("body", i, tk)
            task("tail", NB, TAIL[0])
            for n in range(LAG_V):
                if n < LAG_T:
                    scores_t(NB, n)
                weighted(NB, n)
                if n == LAG_V % T:
                    task("tail", NB, TAIL[1])
            for tk in TAIL[2:]:
                task("tail", NB, tk)

        @block.scalar
        def _(act):
            def squares(i, n):
                r, t = n // T % RING, n % T
                if t == 0:
                    wait_side(act, "body", i, "pool", ("unit", n // T - 2) if n // T > 1 else None)
                act.wait_ge(s_max, i * STEPS + n + 1)
                act.wait_ge(s_sq, i * STEPS + n + 1)
                nc.scalar.activation(junk[:, n % 2, :], ps_s[:, n % 2, :], ACT.Exp, bias=negmax[:, r, t:t + 1],
                                     accum_out=sumsq[:, r, t:t + 1]).then_inc(s_sq, 1)

            def exp_t(i, n):
                act.wait_ge(s_pv, i * STEPS + n + 1)
                for c in range(2):
                    act.wait_ge(s_st, i * (2 * STEPS) + 2 * n + c + 1)
                    nc.scalar.activation(exps[:, n % RING, 512 * c:512 * c + 512], ps_t[:, c, :], ACT.Exp,
                                         scale=0.5).then_inc(s_exp, 1)

            def values_out(phase, i, n):
                act.wait_ge(s_pv, i * STEPS + n + 3)
                j = n // T
                wait_side(act, phase, i, "pe", ("unit", j - 1) if j else None)
                nc.scalar.activation(o_t[:, :], ps_o[:, 0:QC], ACT.Copy).then_inc(s_ot, 1)

            def ident_act(dst, src, **kw):
                return nc.scalar.activation(dst, src, ACT.Identity, **kw)

            def copy(dst, src):
                return nc.scalar.activation(dst, src, ACT.Copy)

            def task(phase, i, tk):
                kind = tk[0]
                if "act" not in ENGINES[kind]:
                    return
                w = lambda of, t: wait_side(act, phase, i, of, t)
                if "pe" in ENGINES[kind]:
                    w("pe", tk)
                if kind == "mrow":
                    j = tk[1]
                    act.wait_ge(s_mrow, i * (U * 48) + 48 * (j + 1))
                    last = copy(mrow[:, :], ps_w[0:3 * T, 0:P // 2].bitcast(BF16))
                elif kind == "snap":
                    w("pool", ("unit", 1))
                    last = nc.scalar.activation(gtmp[:, 0, :], dif_all[:, :, :].rearrange("p u t -> p (u t)"),
                                                ACT.Exp, scale=0.5)
                elif kind == "std":
                    w("pool", ("snap",))
                    for a in range(2):
                        last = nc.scalar.activation(
                            gin[:, :, :, 4 * a + 1].rearrange("p t h -> p h t"),
                            gtmp[:, 3, U * T // 2 * a:U * T // 2 * (a + 1)].rearrange("p (h t) -> p h t", h=H),
                            ACT.Sqrt)
                elif kind == "logit":
                    last = nc.scalar.activation(alpha_w[:, 0, :], ps_w[0:NW, 0:T * H], ACT.Tanh, bias=g3h[:, :],
                                                scale=0.5)
                elif kind in ("attT", "nT"):
                    last = copy(chan[:, 512 * tk[1]:512 * tk[1] + 512], ps_w[:, :])
                elif kind == "attw":
                    last = ident_act(xa[:, CH * tk[1]:CH * tk[1] + CH], ps_w[:, 0:CH], bias=col[:, 1:2])
                elif kind == "fc1":
                    _, c, j = tk
                    if (c, j) == (0, 0):
                        act.wait_ge(s_exw, i * 64 + 64)
                    for q in range(2):
                        f = 2 * j + q
                        last = ident_act(hpre[:, f, CH * c:CH * c + CH], ps_w[:, CH * q:CH * q + CH],
                                         bias=fc1bs[:, f:f + 1])
                elif kind == "gelu1":
                    w("act", ("fc1", NC - 1, 1))
                    for f in range(FC):
                        last = nc.scalar.activation(hpre[:, f, :], hpre[:, f, :], ACT.Gelu)
                elif kind == "fc2":
                    last = ident_act(y[:, CH * tk[1]:CH * tk[1] + CH], ps_w[:, 0:CH], bias=fc2bs[:, :])
                elif kind == "gelu2":
                    w("dve", ("next", 1))
                    last = nc.scalar.activation(z[:, :, :], z[:, :, :], ACT.Gelu)
                elif kind == "embT":
                    last = copy(emb_t[:, 512 * tk[1]:512 * tk[1] + 512], ps_w[:, :])
                elif kind == "e2h":
                    if tk[1] == 0:
                        w("pool", None)
                    last = ident_act(xc[:, 0, 1 + 512 * tk[1]:513 + 512 * tk[1]], ps_w[:, :], bias=col[:, 0:1])
                elif kind in ("conva", "convg"):
                    _, l, c = tk
                    k = CONV.index(tk) // 2
                    if kind == "conva" and k >= 2:
                        w("pool", CONV[2 * (k - 2) + 1])
                    if kind == "conva":
                        last = ident_act(va[:, c % 2, :], ps_w[:, 0:CH], bias=cb[:, 2 * l:2 * l + 1])
                    else:
                        last = nc.scalar.activation(ug[:, c % 2, :], ps_w[:, CH:2 * CH], ACT.Tanh, scale=0.5,
                                                    bias=cb_half[:, 2 * l + 1:2 * l + 2])
                elif kind == "xnT":
                    last = copy(xn_t[:, 512 * tk[1]:512 * tk[1] + 512], ps_w[:, :])
                elif kind == "qk":
                    _, a, which, k = tk
                    at = QK[a].index(tk)
                    if at >= 2:
                        w("pool", QK[a][at - 2])
                    elif phase == "body":
                        w("pool", None)
                    last = ident_act(stage[:, k, :], ps_w[:, :], scale=0.5 if which == 0 else 1.0)
                last.then_inc(side_sem["act"], 1)

            act.wait_ge(s_load, 16 * N_LOADS)
            act.wait_ge(s_init, 3)
            nc.scalar.activation(g3h[:, :], g3b[:, :], ACT.Copy, scale=0.5)
            nc.scalar.activation(cb_half[:, :], cb[:, :], ACT.Copy, scale=0.5).then_inc(s_init, 1)
            act.wait_ge(s_init, 4)
            act.sem_inc(s_sq, 2)
            act.sem_inc(s_exp, 2)
            act.sem_inc(s_mrow, 48)
            for tk in PRE:
                task("pre", 0, tk)
            with act.Fori(0, NB // E) as group, act.Fori(0, E) as e:
                i = group * E + e
                for n in range(0, STEPS, 2):
                    exp_t(i, n)
                    squares(i, n)
                    for tk in STEP[n]:
                        task("body", i, tk)
                    squares(i, n + 1)
                    exp_t(i, n + 1)
                    if (n + 1) % T == LAG_V % T - 1:
                        values_out("body", i, n + 1)
                    for tk in STEP[n + 1]:
                        task("body", i, tk)
            task("tail", NB, TAIL[0])
            for n in range(LAG_V):
                if n < LAG_T:
                    exp_t(NB, n)
                if n % T == LAG_V % T - 1:
                    values_out("tail", NB, n)
            for tk in TAIL[1:]:
                task("tail", NB, tk)

        @block.vector
        def _(dve):
            pos = {"n": 0, "base": 0}

            def chain(i, ins):
                pos["n"] += 1
                ins.then_inc(s_dchain, 1)
                dve.wait_ge(s_dchain, i * pos["per"] + pos["base"] + pos["n"] if pos["loop"] else pos["base"] + pos["n"])

            def row_max(i, n):
                r, t = n // T % RING, n % T
                if t == 0:
                    wait_side(dve, "body", i, "pool", ("unit", n // T - 2) if n // T > 1 else None)
                dve.wait_ge(s_scores, i * STEPS + n + 1)
                nc.vector.tensor_reduce(negmax[:, r, t:t + 1], ps_s[:, n % 2, :], axis=AX, op=ALU.max, negate=True)\
                    .then_inc(s_max, 1)

            def row_min(i, n):
                r, t = n // T % RING, n % T
                dve.wait_ge(s_sq, i * STEPS + n + 3)
                nc.vector.tensor_reduce(rowmin[:, r, t:t + 1], ps_s[:, n % 2, :], axis=AX, op=ALU.min)\
                    .then_inc(s_min, 1)

            def divide(phase, i, j):
                u = (j - 2) % U
                if j == 2:
                    wait_side(dve, phase, i, "pool", ("snap",))
                o = ps_w[:, 0:2 * P].rearrange("p (s b c) -> p b s c", s=2, b=4)
                by_tile = lambda x: x[:, u, :].rearrange("p (b s) -> p b s", s=2)
                chain(i, nc.vector.reciprocal(by_tile(recip), o[:, :, :, HD]))
                nc.vector.tensor_tensor(by_tile(mean_all), o[:, :, :, HD], by_tile(recip), ALU.mult)
                return nc.vector.tensor_tensor(
                    o_all[:, u, :, :].rearrange("p (b s) d -> p b s d", s=2), o[:, :, :, 0:HD],
                    by_tile(recip).unsqueeze(3).to_broadcast([P, 4, 2, HD]), ALU.mult)

            def moments(i, src, k):
                for t in range(T):
                    last = nc.vector.bn_stats(bn[:, t, :], src[:, t, :])
                chain(i, last)
                dve.nop(nofuse=True)
                for t in range(T):
                    last = nc.vector.bn_aggr(mv[:, k, t, :], bn[:, t, :])
                return last

            def task(phase, i, tk):
                kind = tk[0]
                if "dve" not in ENGINES[kind]:
                    return
                w = lambda of, t: wait_side(dve, phase, i, of, t)
                if "pe" in ENGINES[kind]:
                    w("pe", tk)
                four = ps_w[:, :].rearrange("p (q c) -> p q c", q=4)
                if kind == "unit":
                    last = divide(phase, i, tk[1])
                elif kind == "win":
                    last = nc.vector.tensor_copy(winm[:, :], ps_w[0:H * 8, 0:T * NW])
                elif kind == "hid1":
                    last = nc.vector.tensor_scalar(hid1[:, :, :].rearrange("p g w -> p (g w)"), ps_w[:, :],
                                                   g1b[:, :], 0.0, ALU.add, ALU.max)
                elif kind == "hid2":
                    last = nc.vector.tensor_scalar(hid2[:, :, :].rearrange("p g w -> p (g w)"), ps_w[0:4 * HD, :],
                                                   g2b[:, :], 0.0, ALU.add, ALU.max)
                elif kind == "alpha":
                    last = nc.vector.tensor_copy(alpha_q[:, :], ps_w[:, 0:T * H])
                elif kind == "wo":
                    k = 4 * tk[1]
                    if k == 0:
                        w("pool", None)
                    last = nc.vector.tensor_tensor(h2[:, k:k + 4, :], four, h_cur[:, k:k + 4, :], ALU.add)
                elif kind == "ln2":
                    w("dve", ("wo", 1))
                    last = moments(i, h2, 0)
                elif kind == "ln3":
                    w("pool", ("ln2",))
                    last = moments(i, x2, 1)
                elif kind == "next":
                    k = 4 * tk[1]
                    if k == 0:
                        dve.wait_ge(s_out, i * 16 + 16)
                    last = nc.vector.tensor_tensor(z[:, k:k + 4, :], four,
                                                   row[:, 1, :].unsqueeze(1).to_broadcast([P, 4, P]), ALU.add)
                elif kind == "h2e":
                    k = 4 * tk[1]
                    if k == 0 and phase == "body":
                        w("pool", ("hcopy",))
                    last = nc.vector.tensor_tensor(h_next[:, k:k + 4, :], four,
                                                   row[:, 0, :].unsqueeze(1).to_broadcast([P, 4, P]), ALU.add)
                elif kind == "ln1":
                    w("dve", ("h2e", 1))
                    last = moments(i, h_next, 2)
                elif kind == "v":
                    k = 4 * tk[1]
                    if k == 0 and phase == "body":
                        w("pool", ("vcopy", 1))
                    for q in range(4):
                        last = nc.vector.tensor_copy(
                            v_next[:, k + q, :].rearrange("p (h c) -> p h c", h=H)[:, :, 0:HD],
                            four[:, q, :].rearrange("p (h c) -> p h c", h=H))
                last.then_inc(side_sem["dve"], 1)

            for t in (g1, g2, g3):
                last = nc.vector.memset(t[:].rearrange("p a b -> p (a b)") if len(t.shape) == 3 else t[:, :], 0.0)
            last.then_inc(s_init, 1)
            for t in (negmax, rowmin, sumsq):
                nc.vector.memset(t[:, :, :], 0.0)
            for t in (recip, mean_all, sq_all, dif_all):
                nc.vector.memset(t[:, :, :], 0.0)
            nc.vector.memset(exps[:, :, :], 1.0)
            nc.vector.memset(qst[:, :, :], 0.0)
            nc.vector.memset(kst[:, :, :], 0.0)
            nc.vector.memset(rs_pow[:, :], -0.5)
            nc.vector.memset(xc[:, :, 0:1], 0.0)
            last = nc.vector.memset(xc[:, :, L + 1:L + 2], 0.0)
            pos.update(loop=False, base=0, per=0)
            chain(0, last)
            last = nc.vector.memset(kst[KSC:KST, :, :], 1.0)
            last.then_inc(s_init, 1)
            dve.sem_inc(s_min, 2)
            dve.sem_inc(s_out, 16)
            dve.wait_ge(s_load, 16 * N_LOADS)
            dve.wait_ge(s_init, 4)
            for tk in PRE:
                task("pre", 0, tk)
            pos.update(loop=True, base=pos["n"], n=0, per=U + 3)
            with dve.Fori(0, NB // E) as group, dve.Fori(0, E) as e:
                i = group * E + e
                for n in range(0, STEPS, 2):
                    row_max(i, n)
                    row_max(i, n + 1)
                    for tk in STEP[n]:
                        task("body", i, tk)
                    row_min(i, n)
                    row_min(i, n + 1)
                    for tk in STEP[n + 1]:
                        task("body", i, tk)
            assert pos["n"] == pos["per"], pos
            pos.update(n=0)
            for tk in TAIL:
                task("tail", NB, tk)

        @block.gpsimd
        def _(pool):
            pos = {"n": 0, "base": 0, "loop": False, "per": 0}

            def chain(i, ins):
                pos["n"] += 1
                ins.then_inc(s_pchain, 1)
                pool.wait_ge(s_pchain, i * pos["per"] + pos["base"] + pos["n"] if pos["loop"]
                             else pos["base"] + pos["n"])

            tt = nc.gpsimd.tensor_tensor

            def ts(*args):
                pool.nop(nofuse=True)
                return nc.gpsimd.tensor_scalar(*args)

            def copy(dst, src):
                return ts(dst, src, 1.0, 1.0, ALU.mult, ALU.mult)

            def statistics(phase, i, j):
                u = (j - 2) % U
                r = u % RING
                wait_side(pool, phase, i, "dve", ("unit", j))
                pool.wait_ge(s_sq, i * STEPS + max(T * (j - 2) + T + 2, 2))
                if j == 2:
                    wait_side(pool, phase, i, "act", ("snap",))
                tt(dif_all[:, u, :], rowmin[:, r, :], negmax[:, r, :], ALU.add)
                chain(i, tt(sq_all[:, u, :], sumsq[:, r, :], recip[:, u, :], ALU.mult))
                return tt(sq_all[:, u, :], sq_all[:, u, :], recip[:, u, :], ALU.mult)

            def normalise(i, dst, src, k):
                chain(i, ts(rstd[:, k, :], mv[:, k, :, 1], 1.0, EPS, ALU.mult, ALU.add))
                chain(i, tt(rstd[:, k, :], rstd[:, k, :], rs_pow[:, :], ALU.pow))
                chain(i, tt(dst[:, :, :], src[:, :, :], mv[:, k, :, 0].unsqueeze(2).to_broadcast([P, T, P]),
                            ALU.subtract))
                return tt(dst[:, :, :], dst[:, :, :], rstd[:, k, :].unsqueeze(2).to_broadcast([P, T, P]), ALU.mult)

            def task(phase, i, tk):
                kind = tk[0]
                w = lambda of, t: wait_side(pool, phase, i, of, t)
                if kind == "gather":
                    b = 0 if phase == "pre" else i + 1
                    pool.wait_ge(s_idx, 16 if phase == "pre" else i * 16 + 32)
                    w("pe", None)
                    pool.nop(nofuse=True)
                    for t in range(T):
                        nc.gpsimd.indirect_dma_start(out=emb[:, t, :], out_offset=None, in_=table[:, :],
                                                     in_offset=bass.IndirectOffsetOnAxis(ap=idx[:, t:t + 1], axis=0))\
                            .then_inc(s_emb, 16)
                    return
                if "pool" not in ENGINES[kind]:
                    return
                wait_own(pool, phase, i, "pool", tk)
                if kind == "unit":
                    last = statistics(phase, i, tk[1])
                elif kind == "msplit":
                    j = tk[1]
                    r = (j - 1) % RING
                    pool.wait_ge(s_max, i * STEPS + T * j)
                    w("pe", ("mrow", j - 1))
                    chain(i, copy(mparts[:, 0, :], negmax[:, r, :]))
                    chain(i, tt(mrest[:, 0, :], negmax[:, r, :], mparts[:, 0, :], ALU.subtract))
                    chain(i, copy(mparts[:, 1, :], mrest[:, 0, :]))
                    last = tt(mparts[:, 2, :], mrest[:, 0, :], mparts[:, 1, :], ALU.subtract)
                elif kind == "vcopy":
                    if tk[1] == 0:
                        w("dve", None)
                        pool.wait_ge(s_pv, i * STEPS + 2)
                        last = copy(v_cur[:, :, 0:6 * VW], v_next[:, :, 0:6 * VW])
                    else:
                        pool.wait_ge(s_pv, i * STEPS + LAG_V - 1 + 3)
                        last = copy(v_cur[:, :, 6 * VW:H * VW], v_next[:, :, 6 * VW:])
                elif kind == "hcopy":
                    w("dve", ("wo", 1))
                    last = copy(h_cur[:, :, :], h_next[:, :, :])
                elif kind == "snap":
                    if phase == "body":
                        w("pe", None)
                    oa = o_all[:, :, :, :].rearrange("p u t d -> p t u d")
                    heads = lambda t: t[:, :, :].rearrange("p t (h d) -> p t h d", h=H)
                    tt(heads(odif), oa[:, :, 0:H, :], oa[:, :, H:U, :], ALU.subtract)
                    copy(heads(o2), oa[:, :, H:U, :])
                    flat = lambda t: t[:, :, :].rearrange("p u t -> p (u t)")

                    def feature(f, fn):
                        for a in range(2):
                            last = fn(gin[:, :, :, 4 * a + f].rearrange("p t h -> p h t"), a)
                        return last

                    def of(src, a):
                        return src[:, H * a:H * a + H, :]

                    def of2(k, a):
                        return gtmp[:, k, U * T // 2 * a:U * T // 2 * (a + 1)].rearrange("p (h t) -> p h t", h=H)
                    feature(0, lambda dst, a: ts(dst, of(mean_all, a), 1.0 / L, 1.0, ALU.mult, ALU.mult))
                    feature(2, lambda dst, a: copy(dst, of(recip, a)))
                    chain(i, tt(gtmp[:, 1, :], flat(mean_all), flat(mean_all), ALU.mult))
                    chain(i, ts(gtmp[:, 2, :], gtmp[:, 1, :], 1.0 / L, 1.0, ALU.mult, ALU.mult))
                    chain(i, tt(gtmp[:, 1, :], flat(sq_all), gtmp[:, 2, :], ALU.subtract))
                    chain(i, ts(gtmp[:, 3, :], gtmp[:, 1, :], 1.0 / (L - 1), 0.0, ALU.mult, ALU.max))
                    w("act", tk)
                    last = feature(3, lambda dst, a: tt(dst, of2(0, a), of(recip, a), ALU.mult))
                elif kind == "logit":
                    w("act", tk)
                    last = ts(alpha_w[:, 1, :], alpha_w[:, 0, :], 0.5, 0.5, ALU.mult, ALU.add)
                elif kind == "alpha":
                    w("dve", tk)
                    flat = lambda t: t[:, :, :].rearrange("p t (h d) -> p (t h) d", h=H)
                    chain(i, tt(flat(att), flat(odif), alpha_q[:, :].unsqueeze(2).to_broadcast([P, T * H, HD]),
                                ALU.mult))
                    last = tt(flat(att), flat(att), flat(o2), ALU.add)
                elif kind == "ln2":
                    w("dve", tk)
                    last = normalise(i, x2, h2, 0)
                elif kind == "ln3":
                    w("dve", tk)
                    w("pe", ("attT", 1))
                    chain(i, normalise(i, att, x2, 1))
                    chain(i, tt(att[:, :, :], att[:, :, :], row[:, 2, :].unsqueeze(1).to_broadcast([P, T, P]),
                                ALU.mult))
                    last = tt(att[:, :, :], att[:, :, :], row[:, 3, :].unsqueeze(1).to_broadcast([P, T, P]), ALU.add)
                elif kind == "gelu2":
                    w("act", tk)
                    last = tt(z[:, :, :], z[:, :, :], h2[:, :, :], ALU.add)
                elif kind == "convg":
                    _, l, c = tk
                    w("act", tk)
                    x_in = xc[:, l % 2, 1 + CH * c:1 + CH * c + CH]
                    x_out = xc[:, (l + 1) % 2, 1 + CH * c:1 + CH * c + CH]
                    ts(ctmp[:, 3, :], x_in, RES, 1.0, ALU.mult, ALU.mult)
                    chain(i, tt(ctmp[:, 0, :], ug[:, c % 2, :], va[:, c % 2, :], ALU.mult))
                    chain(i, tt(ctmp[:, 1, :], ctmp[:, 0, :], va[:, c % 2, :], ALU.add))
                    chain(i, ts(ctmp[:, 2, :], ctmp[:, 1, :], 0.5, RES, ALU.mult, ALU.mult))
                    last = tt(x_out, ctmp[:, 2, :], ctmp[:, 3, :], ALU.add)
                elif kind == "ln1":
                    w("dve", tk)
                    last = normalise(i, xn, h_next, 2)
                elif kind == "qk":
                    _, a, which, k = tk
                    w("act", tk)
                    dst = part[:, a, which, :, 512 * k:512 * k + 512]
                    chain(i, copy(dst[:, 0, :], stage[:, k, :]))
                    chain(i, tt(srest, stage[:, k, :], dst[:, 0, :], ALU.subtract))
                    chain(i, copy(dst[:, 1, :], srest))
                    last = tt(dst[:, 2, :], srest, dst[:, 1, :], ALU.subtract)
                last.then_inc(side_sem["pool"], 1)

            for t in (v_next, v_cur, h_cur):
                nc.gpsimd.memset(t[:, :, :], 0.0)
            nc.gpsimd.memset(mparts[:, :, :], 0.0)
            last = nc.gpsimd.memset(o_all[:, :, :, :], 0.0)
            chain(0, last)
            for t in (v_next, v_cur):
                last = nc.gpsimd.memset(t[:, :, 0:H * VW].rearrange("p t (h c) -> p t h c", c=VW)[:, :, :, HD:VW],
                                        1.0)
            pool.wait_ge(s_load, 16 * N_LOADS)
            nc.gpsimd.tensor_scalar(ident_b[:, :], ident, 1.0, 1.0, ALU.mult, ALU.mult).then_inc(s_init, 1)
            pool.sem_inc(s_pv, 2)
            pool.wait_ge(s_init, 4)
            for tk in PRE:
                task("pre", 0, tk)
            per = 0
            for tk in BODY:
                per += {"msplit": 3, "unit": 1, "snap": 4, "alpha": 1, "ln2": 3, "ln3": 5, "convg": 3, "ln1": 3, "qk": 3}.get(tk[0], 0)
            pos.update(loop=True, base=pos["n"], n=0, per=per)
            with pool.Fori(0, NB // E) as group, pool.Fori(0, E) as e:
                i = group * E + e
                for n in range(STEPS):
                    for tk in STEP[n]:
                        task("body", i, tk)
            assert pos["n"] == pos["per"], pos
            pos.update(n=0)
            for tk in TAIL:
                task("tail", NB, tk)


def _constants():
    c = np.zeros((P, P + NW + P), np.float32)
    c[:, 0:P] = np.eye(P)
    for q in range(P):
        c[q, P + q // WS] = 1.0 / WS
        c[q // WS, P + NW + q] = 1.0
    return c


def kernel(**inputs):
    import concourse.bacc as _bacc
    from concourse.bass_utils import run_bass_kernel_spmd as _run

    a = {k: np.asarray(v) for k, v in inputs.items()}
    nb = a["x"].shape[0]
    ids = np.zeros((nb + 1, P, T), np.int32)
    ids[:nb] = a["x"].reshape(nb, T, P).transpose(0, 2, 1)
    f = {k[3:]: v for k, v in a.items() if k.startswith("L0_")}
    before = [(e - 1) % E for e in range(E)]
    arrays = {
        "ids": ids, "table": f["tok_emb_table"], "consts": _constants(),
        "w_e2h": f["tok_W_e2h"], "b_e2h": f["tok_b_e2h"].reshape(P, 1),
        "conv_w": f["tok_conv_w"].transpose(2, 0, 3, 1),
        "conv_b": f["tok_conv_b"].reshape(2 * LAYERS, P).T,
        "w_h2e": f["tok_W_h2e"], "b_h2e": f["tok_b_h2e"].reshape(1, P),
        "wq1": f["attn_Wq1"], "wk1": f["attn_Wk1"], "wq2": f["attn_Wq2"], "wk2": f["attn_Wk2"],
        "wv": f["attn_Wv"], "wo": f["attn_Wo"],
        "gw1": f["attn_gw1"], "gb1": f["attn_gb1"].reshape(-1, 1), "gw2": f["attn_gw2"],
        "gb2": f["attn_gb2"].reshape(-1, 1), "gw3": f["attn_gw3"], "gb3": f["attn_gb3"].reshape(1, 1),
        "ln_g": f["ffn_ln_g"].reshape(1, P), "ln_b": f["ffn_ln_b"].reshape(1, P),
        "attn_w": f["ffn_attn_w"].T, "attn_b": f["ffn_attn_b"].reshape(P, 1),
        "fc1_w": f["ffn_fc1_w"].transpose(0, 2, 1)[before],
        "fc1_b": f["ffn_fc1_b"].reshape(E, FC, P).transpose(0, 2, 1)[before],
        "fc2_w": f["ffn_fc2_w"].reshape(E, P, FC, P).transpose(0, 3, 2, 1)[before],
        "fc2_b": f["ffn_fc2_b"].reshape(E, P, 1)[before],
        "next_w": f["ffn_next_w"].T, "next_b": f["ffn_next_b"].reshape(1, P),
    }
    nc = _bacc.Bacc("TRN2", target_bir_lowering=False, num_devices=1)
    feed, args = {}, {}
    for name, v in arrays.items():
        v = np.ascontiguousarray(v)
        feed[f"in_{name}"] = v
        args[name] = nc.dram_tensor(f"in_{name}", v.shape, mybir.dt.from_np(v.dtype), kind="ExternalInput").ap()
    store = nc.dram_tensor("out_dram", (nb + 1, T, P, P), F32, kind="ExternalOutput").ap()
    tower_kernel(nc, out=store.rearrange("b t p d -> b p t d"), **args)
    r = _run(nc, [feed], core_ids=[0])
    return np.asarray(r.results[0]["out_dram"])[1:].reshape(nb, L, P)
```

```python
from contextlib import ExitStack

import numpy as np

import concourse.bass as bass
from concourse import mybir

F32 = mybir.dt.float32
BF16 = mybir.dt.bfloat16
I32 = mybir.dt.int32
ALU = mybir.AluOpType
ACT = mybir.ActivationFunctionType
AX = mybir.AxisListType.X

P = 128
L = 1024
T = L // P
H = 8
HD = P // H
VW = HD + 1
U = 2 * H
STEPS = U * T
E = 8
FC = 4
WS = 4
NW = P // WS
LAYERS, TAPS = 6, 3
RING = 4
NPART = 6
KSC = NPART * HD
KST = KSC + 3
Q_PART = (0, 0, 0, 1, 1, 2)
K_PART = (0, 1, 2, 0, 1, 0)
LAG_T = T + 4
LAG_V = LAG_T + 2
CH = 256
NC = L // CH
RES = 0.7071067811865476
EPS = 1e-5
QC = L // 4

def two(kind):
    return [(kind, 0), (kind, 1)]


CONV = [("conv" + half, l, c) for l in range(LAYERS) for c in range(NC) for half in "ag"]
QK = [[("qk", a, w, k) for w in range(2) for k in range(2)] for a in range(2)]
PRE = [("gather",)] + two("embT") + two("e2h") + CONV + two("h2e") + [("ln1",)] + two("xnT") + QK[0] + two("v")
POST = ([("snap",), ("std",), ("win",), ("hid1",), ("hid2",), ("logit",), ("alpha",)] + two("attT") + two("wo")
        + [("ln2",), ("ln3",)] + two("nT") + [("attw", c) for c in range(NC)]
        + [("fc1", c, j) for c in range(NC) for j in range(2)] + [("gelu1",)]
        + [("fc2", c) for c in range(NC)] + two("next") + [("gelu2",)])
ENGINES = {
    "msplit": ("pool",), "mrow": ("dve",), "unit": ("dve", "pool"), "vcopy": ("pool",), "hcopy": ("pool",), "snap": ("pool", "act"),
    "std": ("act",),
    "win": ("pe", "dve"), "hid1": ("pe", "dve"), "hid2": ("pe", "dve"), "logit": ("pe", "act", "pool"),
    "alpha": ("pe", "dve", "pool"), "attT": ("pe", "act"), "wo": ("pe", "dve"), "ln2": ("dve", "pool"),
    "ln3": ("dve", "pool"), "nT": ("pe", "act"), "attw": ("pe", "act"), "fc1": ("pe", "act"), "gelu1": ("act",),
    "fc2": ("pe", "act"), "next": ("pe", "dve"), "gelu2": ("act", "pool"), "gather": (), "embT": ("pe", "act"),
    "e2h": ("pe", "act"), "conva": ("pe", "act"), "convg": ("pe", "act", "pool"), "h2e": ("pe", "dve"),
    "ln1": ("dve", "pool"), "xnT": ("pe", "act"), "qk": ("pe", "act", "pool"), "v": ("pe", "dve"),
}
READER = {k: ("dve" if "dve" in v else "act") for k, v in ENGINES.items() if "pe" in v}


COST = {"win": 5, "hid1": 9, "hid2": 9, "logit": 8, "alpha": 3, "attT": 4, "wo": 9, "nT": 4,
        "attw": 7, "fc1": 9, "fc2": 18, "next": 9, "embT": 4, "e2h": 9, "conva": 13, "convg": 13, "h2e": 9, "xnT": 4,
        "qk": 9, "v": 9}
POOL_COST = {"msplit": 8, "unit": 5, "qk": 35, "convg": 23, "gather": 85, "snap": 80, "alpha": 46, "hcopy": 20,
             "ln1": 66, "ln2": 66, "ln3": 66, "gelu2": 24, "vcopy": 15}
STEP_WEIGHT = 27
GAP = {("std",): 5, ("win",): 2, ("hid1",): 2, ("hid2",): 2, ("logit",): 2, ("alpha",): 2, ("attT", 0): 4,
       ("wo", 0): 2, ("ln3",): 5, ("nT", 0): 6, ("attw", 0): 2, ("gelu1",): 1, ("fc2", 0): 4, ("next", 0): 2,
       ("embT", 0): 1, ("e2h", 0): 2, ("conva", 0, 0): 2, ("h2e", 1): 3, ("ln1",): 2, ("xnT", 0): 5,
       **{task: 2 for task in QK[0]}}

SPREAD = {"attw": 2, "fc1": 2}


SLOTS = {"ln1": (2, 3, 4), "ln2": (0, 1, 2, 3, 4), "ln3": (0, 1, 2, 3), "alpha": (0, 1, 2, 3, 4),
         "gelu2": (0, 1, 2, 3, 4), "snap": (0, 1), "hcopy": (0, 1, 2, 3, 4)}


def plan():
    at = {n: [] for n in range(STEPS)}
    for j in range(U):
        at[j * T].append(("mrow", j))
        at[j * T + LAG_V % T - 1].append(("unit", j))
    for n, task in {0: ("gather",), 2: ("vcopy", 0), 3: QK[1][0], 5: QK[1][1], 8: QK[1][2], 10: QK[1][3],
                    14: ("vcopy", 1)}.items():
        at[n].append(task)
    post, pre = [list(POST), T + LAG_V % T + 2], [list(PRE[1:]), T - 2]
    cost = lambda tasks: sum(COST.get(t[0], 0) for t in tasks)
    share = cost(BODY_TASKS) / (STEPS - 2 * T)
    behind = 0
    for n in range(STEPS):
        behind = max(behind - STEP_WEIGHT, 0) + sum(POOL_COST.get(t[0], 0) for t in at[n])
        for stage in (post, pre):
            tasks, first = stage
            while tasks and first <= n and n % T in SLOTS.get(tasks[0][0], range(T)):
                task = tasks[0]
                done = cost([t for m in range(n) for t in at[m]])
                on_pe = task[0] in COST
                if on_pe and (cost(at[n]) or stage is pre and done + COST[task[0]] / 2 > share * (n + 1)):
                    break
                if task[0] in ("conva", "convg") and behind > STEP_WEIGHT:
                    break
                if stage is pre and any(t[0] in ("gelu1", "gelu2", "std") for t in at[n]):
                    break
                at[n].append(tasks.pop(0))
                behind += POOL_COST.get(task[0], 0)
                if task == ("wo", 1):
                    at[n].append(("hcopy",))
                first = n + (GAP.get(tasks[0], SPREAD.get(tasks[0][0], 1)) if tasks else 0)
            stage[1] = first
    assert not post[0] and not pre[0], (post, pre)
    for j in range(1, U + 1):
        at[j * T - 2].append(("msplit", j))
    return at


BODY_TASKS = [("mrow", j) for j in range(U)] + [("unit", j) for j in range(U)] + QK[1] + POST + PRE
STEP = plan()
BODY = [task for n in range(STEPS) for task in STEP[n]]
TAIL = [("mrow", 0), ("unit", 0), ("unit", 1)] + POST
PHASES = {"pre": PRE, "body": BODY, "tail": TAIL}


class Side:

    def __init__(self, sems):
        self.sems = sems

    def upto(self, phase, i, eng, task):
        tasks = PHASES[phase]
        n = 0 if task is None else tasks.index(task) + 1
        count = sum(eng in ENGINES[t[0]] for t in tasks[:n])
        if phase == "pre":
            return count
        count += sum(eng in ENGINES[t[0]] for t in PRE)
        return i * sum(eng in ENGINES[t[0]] for t in BODY) + count


def tower_kernel(nc, ids, table, consts, w_e2h, b_e2h, conv_w, conv_b, w_h2e, b_h2e, wq1, wk1, wq2, wk2, wv, wo,
                 gw1, gb1, gw2, gb2, gw3, gb3, ln_g, ln_b, attn_w, attn_b, fc1_w, fc1_b, fc2_w, fc2_b,
                 next_w, next_b, out):
    NB = ids.shape[0] - 1

    with ExitStack() as ctx:
        def sb(name, shape, dt=F32):
            return ctx.enter_context(nc.sbuf_tensor(name, shape, dt))

        def sem(name):
            return ctx.enter_context(nc.semaphore(name))

        ps_s = ctx.enter_context(nc.psum_tensor("ps_s", [P, 2, L], F32))
        ps_t = ctx.enter_context(nc.psum_tensor("ps_t", [P, 2, 512], F32))
        ps_o = ctx.enter_context(nc.psum_tensor("ps_o", [P, 512], F32))
        ps_w = ctx.enter_context(nc.psum_tensor("ps_w", [P, 512], F32))

        cst = sb("cst", [P, P + NW + P])
        ident = cst[:, 0:P]
        win_mean = cst[:, P:P + NW]
        win_rep = cst[0:NW, P + NW:P + NW + P]
        cw = sb("cw", [P, LAYERS, TAPS, 2 * P])
        cb = sb("cb", [P, 2 * LAYERS])
        cb_half = sb("cb_half", [P, 2 * LAYERS])
        we2h, wh2e = sb("we2h", [P, P]), sb("wh2e", [P, P])
        wqk = sb("wqk", [P, 2, 2, P])
        wv_s, wo_s, wattn, wnext = sb("wv_s", [P, P]), sb("wo_s", [P, P]), sb("wattn", [P, P]), sb("wnext", [P, P])
        col = sb("col", [P, 4])
        row = sb("row", [P, 2, P])
        g1 = sb("g1", [H * 8, 2, P])
        g2 = sb("g2", [P, 4 * HD])
        g3 = sb("g3", [4 * HD, 4])
        g1b, g2b = sb("g1b", [P, 1]), sb("g2b", [4 * HD, 1])
        g3b, g3h = sb("g3b", [NW, 1]), sb("g3h", [NW, 1])
        rs_pow = sb("rs_pow", [P, T])

        part = sb("part", [P, 2, 2, 3, L], BF16)
        qst = sb("qst", [KST, RING, L], BF16)
        kst = sb("kst", [KST, RING, L], BF16)
        exps = sb("exps", [P, RING, L])
        junk = sb("junk", [P, 2, L], BF16)
        negmax, rowmin, sumsq = (sb(n, [P, RING, T]) for n in ("negmax", "rowmin", "sumsq"))
        mparts = sb("mparts", [P, 4, T], BF16)
        mrest = sb("mrest", [P, 2, T])
        mrow = sb("mrow", [P, 32], BF16)
        v_next, v_cur = sb("v_next", [P, T, H * VW]), sb("v_cur", [P, T, H * VW + 32 - VW])
        o_t = sb("o_t", [P, QC])
        o_all = sb("o_all", [P, U, T, HD])
        recip, mean_all, sq_all, dif_all = (sb(n, [P, U, T]) for n in ("recip", "mean_all", "sq_all", "dif_all"))

        gin = sb("gin", [P, T, H, 8])
        gtmp = sb("gtmp", [P, 4, U * T])
        winm = sb("winm", [H * 8, T * NW])
        hid1 = sb("hid1", [P, 2, T * NW])
        hid2 = sb("hid2", [4 * HD, 2, T * NW])
        alpha_w = sb("alpha_w", [NW, 2, T * H])
        alpha_q = sb("alpha_q", [P, T * H])
        odif, o2 = sb("odif", [P, T, P]), sb("o2", [P, T, P])
        att = sb("att", [P, T, P])
        chan = sb("chan", [P, L])
        h_next, h_cur, h2 = sb("h_next", [P, T, P]), sb("h_cur", [P, T, P]), sb("h2", [P, T, P])
        x2 = sb("x2", [P, T, P])
        bn = sb("bn", [P, T, 6])
        mv = sb("mv", [P, 3, T, 2])
        rstd = sb("rstd", [P, 3, T])
        xa = sb("xa", [P, L])
        hpre = sb("hpre", [P, FC, L])
        y = chan
        z = sb("z", [P, T, P])
        fc1s, fc2s = sb("fc1s", [P, FC * P]), sb("fc2s", [P, FC, P])
        fc1bs, fc2bs = sb("fc1bs", [P, FC]), sb("fc2bs", [P, 1])

        idx = sb("idx", [P, T], I32)
        xc = sb("xc", [P, 2, L + 2])
        va, ug = sb("va", [P, 2, CH]), sb("ug", [P, 2, CH])
        ctmp = sb("ctmp", [P, 4, CH])
        xn = sb("xn", [P, T, P])
        xn_t = sb("xn_t", [P, L])
        emb, emb_t = att, chan
        stage = sb("stage", [P, 2, 512])
        srest = ctmp[:, 0:2, :].rearrange("p a b -> p (a b)")

        s_load = sem("s_load")
        s_init = sem("s_init")
        s_scores = sem("s_scores")
        s_max = sem("s_max")
        s_min = sem("s_min")
        s_sq = sem("s_sq")
        s_st = sem("s_st")
        s_exp = sem("s_exp")
        s_pv = sem("s_pv")
        s_ot = sem("s_ot")
        s_ring = [sem(f"s_ring{r}") for r in range(RING)]
        s_mrow = sem("s_mrow")
        s_idx = sem("s_idx")
        s_emb = sem("s_emb")
        s_exw = sem("s_exw")
        s_out = sem("s_out")
        s_dchain = sem("s_dchain")
        s_pchain = sem("s_pchain")
        side_sem = {e: sem("side_" + e) for e in ("pe", "act", "dve", "pool")}
        side = Side(side_sem)

        def wait_side(eng, phase, i, of, task=None):
            eng.wait_ge(side_sem[of], side.upto(phase, i, of, task))

        def bank_of(phase, task):
            users = [t for t in PHASES[phase] if t[0] in READER]
            if phase == "body" or task not in users:
                return ps_w[:, :]
            return (ps_w[:, :], ps_t[:, 0, :], ps_t[:, 1, :])[users.index(task) % 3]

        def wait_bank(eng, phase, i, task):
            users = [t for t in PHASES[phase] if t[0] in READER]
            at = users.index(task) - (1 if phase == "body" else 3)
            if at >= 0:
                wait_side(eng, phase, i, READER[users[at][0]], users[at])
            elif phase != "pre":
                wait_side(eng, phase, i, "act")
                wait_side(eng, phase, i, "dve")

        def wait_own(eng, phase, i, name, task):
            tasks = PHASES[phase]
            before = [t for t in tasks[:tasks.index(task)] if name in ENGINES[t[0]]]
            if before or phase != "pre":
                wait_side(eng, phase, i, name, before[-1] if before else None)

        weight_loads = [(cst[:, :], consts), (we2h[:, :], w_e2h), (cw[:, :, :, :], conv_w), (cb[:, :], conv_b),
                        (wh2e[:, :], w_h2e), (wqk[:, 0, 0, :], wq1), (wqk[:, 0, 1, :], wk1), (wqk[:, 1, 0, :], wq2),
                        (wqk[:, 1, 1, :], wk2), (wv_s[:, :], wv), (wo_s[:, :], wo), (wattn[:, :], attn_w),
                        (wnext[:, :], next_w)]
        weight_loads += [(col[:, k:k + 1], b) for k, b in enumerate((b_e2h, attn_b, ln_g, ln_b))]
        weight_loads += [(row[:, k, :], b.to_broadcast([P, P])) for k, b in enumerate((b_h2e, next_b))]
        gate_loads = [(g1[8 * h:8 * h + 8, h // 4, 32 * (h % 4):32 * (h % 4) + 32], gw1) for h in range(H)]
        for j in range(4):
            gate_loads += [(g2[32 * j:32 * j + 32, HD * j:HD * j + HD], gw2), (g3[HD * j:HD * j + HD, j:j + 1], gw3),
                           (g1b[32 * j:32 * j + 32, :], gb1), (g2b[HD * j:HD * j + HD, :], gb2)]
        gate_loads.append((g3b[:, :], gb3.to_broadcast([NW, 1])))
        N_LOADS = len(weight_loads) + len(gate_loads)

        block = ctx.enter_context(nc.Block())

        @block.sync
        def _(sp):
            def settle():
                sp.nop(nofuse=True)

            def load_ids(b):
                sp.dma_start(idx[:, :], ids[b]).then_inc(s_idx, 16)

            def load_unit(u):
                a, h, r = u // H, u % H, u % RING
                for g in range(NPART):
                    for dst, w, c in ((qst, 0, Q_PART[g]), (kst, 1, K_PART[g])):
                        sp.dma_start(dst[HD * g:HD * g + HD, r, :], part[HD * h:HD * h + HD, a, w, c, :])\
                          .then_inc(s_ring[r], 16)

            def store_mrow(phase, i, j):
                wait_side(sp, phase, i, "dve", ("mrow", j))
                settle()
                for b in range(4):
                    sp.dma_start(qst[KSC:KST, (j - 1) % RING, :].rearrange("c (t b q) -> c t b q", t=T, b=4)[:, :, b, :],
                                 mrow[32 * b:32 * b + 3 * T, :]).then_inc(s_mrow, 16)

            def load_expert(phase, i, e):
                wait_side(sp, phase, i, "pe")
                settle()
                wait_side(sp, phase, i, "act")
                settle()
                for dst, src in ((fc1s[:, :], fc1_w[e]), (fc2s[:, :, :], fc2_w[e]), (fc1bs[:, :], fc1_b[e]),
                                 (fc2bs[:, :], fc2_b[e])):
                    sp.dma_start(dst, src).then_inc(s_exw, 16)

            def store_out(phase, i):
                wait_side(sp, phase, i, "pool", ("gelu2",))
                settle()
                sp.dma_start(out[i], z[:, :, :]).then_inc(s_out, 16)

            load_ids(0)
            for dst, src in weight_loads:
                sp.dma_start(dst, src).then_inc(s_load, 16)
            wait_side(sp, "pre", 0, "pool", QK[0][-1])
            load_unit(0)
            with sp.Fori(0, NB // E) as group, sp.Fori(0, E) as e:
                i = group * E + e
                sp.wait_ge(s_emb, i * (16 * T) + 16 * T)
                settle()
                load_ids(i + 1)
                load_expert("body", i, e)
                for j in range(U):
                    if j:
                        sp.wait_ge(s_st, i * (2 * STEPS) + 2 * (T * (j - 3) + T - 1 + LAG_T) + 2)
                    else:
                        sp.wait_ge(s_exp, i * (2 * STEPS) + 2)
                    settle()
                    store_mrow("body", i, j)
                    if j + 1 in (U // 2, U):
                        wait_side(sp, "body", i, "pool", QK[(j + 1) % U // H][-1])
                        settle()
                    load_unit((j + 1) % U)
                    if ("gelu2",) in sum((STEP[n] for n in range(j * T, j * T + T)), []):
                        store_out("body", i)
            load_expert("tail", NB, 0)
            store_mrow("tail", NB, 0)
            store_out("tail", NB)
            sp.wait_ge(s_out, 16 * (NB + 2))

        @block.tensor
        def _(pe):
            def mm(dst, lhs, rhs, start=True, stop=True, **kw):
                return nc.tensor.matmul(dst, lhs, rhs, start=start, stop=stop, **kw)

            def scores(i, n):
                u, t = n // T, n % T
                if t == 0:
                    pe.wait_ge(s_ring[u % RING], i * (4 * 12 * 16) + 12 * 16 * (u // RING + 1))
                pe.wait_ge(s_min, i * STEPS + n + 1)
                for c in range(2):
                    last = mm(ps_s[:, n % 2, 512 * c:512 * c + 512], qst[0:KSC, u % RING, P * t:P * t + P],
                              kst[0:KSC, u % RING, 512 * c:512 * c + 512])
                last.then_inc(s_scores, 1)

            def scores_t(i, n):
                m = (n - LAG_T) % STEPS
                u, t = m // T, m % T
                if t == 0:
                    pe.wait_ge(s_mrow, i * (U * 64) + 64 * (n // T + 2))
                for c in range(2):
                    pe.wait_ge(s_exp, i * (2 * STEPS) + 2 * n + c + 1)
                    mm(ps_t[:, c, :], kst[:, u % RING, P * t:P * t + P], qst[:, u % RING, 512 * c:512 * c + 512])\
                        .then_inc(s_st, 1)

            def weighted(i, n, count=True):
                m = (n - LAG_V) % STEPS
                h, t = m // T % H, m % T
                if count:
                    pe.wait_ge(s_exp, i * (2 * STEPS) + max(2 * n, 1))
                    if t == 0:
                        pe.wait_ge(s_ot, i * U + n // T + 1)
                    if m == 0:
                        wait_side(pe, "body", i, "pool", ("vcopy", 0))
                    if m == 6 * T:
                        wait_side(pe, "body", i, "pool", ("vcopy", 1))
                blocks = exps[:, (n - 2) % RING, :].rearrange("p (t q c) -> p q t c", t=T, q=4)
                for q in range(4):
                    last = mm(ps_o[32 * q:32 * q + 32, 0:QC], v_cur[:, t, VW * h:VW * h + 32],
                              blocks[:, q], start=(t == 0), stop=(t == T - 1))
                if count:
                    last.then_inc(s_pv, 1)

            def turn(bank, src, k):
                for q in range(4):
                    last = nc.tensor.transpose(bank[:, P * q:P * q + P], src[:, 4 * k + q, :], ident)
                return last

            def task(phase, i, tk):
                kind = tk[0]
                if "pe" not in ENGINES[kind]:
                    return
                wait_bank(pe, phase, i, tk)
                bank = bank_of(phase, tk)
                w = lambda of, t: wait_side(pe, phase, i, of, t)
                if kind == "win":
                    w("act", ("std",))
                    for t in range(T):
                        last = mm(bank[0:H * 8, NW * t:NW * t + NW], gin[:, t, :, :].rearrange("p h f -> p (h f)"),
                                  win_mean)
                elif kind == "hid1":
                    w("dve", ("win",))
                    for g in range(2):
                        last = mm(bank[:, CH * g:CH * g + CH], g1[:, g, :], winm[:, :])
                elif kind == "hid2":
                    w("dve", ("hid1",))
                    for g in range(2):
                        last = mm(bank[0:4 * HD, CH * g:CH * g + CH], g2[:, :], hid1[:, g, :])
                elif kind == "logit":
                    w("dve", ("hid2",))
                    pe.nop(nofuse=True)
                    for t in range(T):
                        for g in range(2):
                            last = mm(bank[0:NW, H * t + 4 * g:H * t + 4 * g + 4],
                                      hid2[:, g, NW * t:NW * t + NW], g3[:, :])
                elif kind == "alpha":
                    w("pool", ("logit",))
                    last = mm(bank[:, 0:T * H], win_rep, alpha_w[:, 1, :])
                elif kind == "attT":
                    w("pool", ("alpha",))
                    last = turn(bank, att, tk[1])
                elif kind == "wo":
                    w("act", ("attT", tk[1]))
                    for q in range(4):
                        t = 4 * tk[1] + q
                        last = mm(bank[:, P * q:P * q + P], chan[:, P * t:P * t + P], wo_s[:, :])
                elif kind == "nT":
                    w("pool", ("ln3",))
                    last = turn(bank, att, tk[1])
                elif kind == "attw":
                    c = tk[1]
                    w("act", ("nT", c // 2))
                    mm(bank[:, 0:CH], wattn[:, :], chan[:, CH * c:CH * c + CH], stop=False, skip_group_check=True)
                    for q in range(2):
                        last = mm(bank[:, P * q:P * q + P], x2[:, 2 * c + q, :], ident, start=False,
                                  skip_group_check=True)
                elif kind == "fc1":
                    _, c, j = tk
                    if (c, j) == (0, 0):
                        pe.wait_ge(s_exw, i * 64 + 64)
                    w("act", ("attw", c))
                    for q in range(2):
                        f = 2 * j + q
                        last = mm(bank[:, CH * q:CH * q + CH], fc1s[:, P * f:P * f + P], xa[:, CH * c:CH * c + CH])
                elif kind == "fc2":
                    c = tk[1]
                    w("act", ("gelu1",))
                    for f in range(FC):
                        last = mm(bank[:, 0:CH], fc2s[:, f, :], hpre[:, f, CH * c:CH * c + CH], start=(f == 0),
                                  stop=(f == FC - 1))
                elif kind == "next":
                    w("act", ("fc2", 2 * tk[1] + 1))
                    for q in range(4):
                        t = 4 * tk[1] + q
                        last = mm(bank[:, P * q:P * q + P], y[:, P * t:P * t + P], wnext[:, :])
                elif kind == "embT":
                    pe.wait_ge(s_emb, (16 * T) if phase == "pre" else (i + 2) * (16 * T))
                    last = turn(bank, emb, tk[1])
                elif kind == "e2h":
                    w("act", ("embT", tk[1]))
                    last = mm(bank[:, :], we2h[:, :], emb_t[:, 512 * tk[1]:512 * tk[1] + 512])
                elif kind in ("conva", "convg"):
                    _, l, c = tk
                    if l == 0:
                        w("act", ("e2h", min((CH * c + CH) // 512, 1)))
                    else:
                        w("pool", ("convg", l - 1, min(c + 1, NC - 1)))
                    g = kind == "convg"
                    for k in range(TAPS):
                        last = mm(bank[:, CH * g:CH * g + CH], cw[:, l, k, P * g:P * g + P],
                                  xc[:, l % 2, CH * c + k:CH * c + k + CH], start=(k == 0), stop=(k == TAPS - 1))
                elif kind == "h2e":
                    w("pool", ("convg", LAYERS - 1, NC // 2 * (tk[1] + 1) - 1))
                    for q in range(4):
                        t = 4 * tk[1] + q
                        last = mm(bank[:, P * q:P * q + P], xc[:, 0, 1 + P * t:1 + P * t + P], wh2e[:, :])
                elif kind == "xnT":
                    w("pool", ("ln1",))
                    last = turn(bank, xn, tk[1])
                elif kind == "qk":
                    _, a, which, k = tk
                    if a == 0:
                        w("act", ("xnT", k))
                    last = mm(bank[:, :], wqk[:, a, which, :], xn_t[:, 512 * k:512 * k + 512])
                elif kind == "v":
                    w("act", ("xnT", tk[1]))
                    for q in range(4):
                        t = 4 * tk[1] + q
                        last = mm(bank[:, P * q:P * q + P], xn_t[:, P * t:P * t + P], wv_s[:, :])
                last.then_inc(side_sem["pe"], 1)

            pe.wait_ge(s_load, 16 * N_LOADS)
            pe.wait_ge(s_init, 3)
            for n in range(-((-LAG_V) % T), 0):
                weighted(0, n, count=False)
            for tk in PRE:
                task("pre", 0, tk)
            wait_side(pe, "body", 0, "act")
            wait_side(pe, "body", 0, "dve")
            with pe.Fori(0, NB // E) as group, pe.Fori(0, E) as e:
                i = group * E + e
                for n in range(0, STEPS, 2):
                    scores(i, n)
                    scores_t(i, n)
                    scores(i, n + 1)
                    for tk in STEP[n]:
                        task("body", i, tk)
                    scores_t(i, n + 1)
                    weighted(i, n)
                    weighted(i, n + 1)
                    for tk in STEP[n + 1]:
                        task("body", i, tk)
            for n in range(LAG_V):
                if n < LAG_T:
                    scores_t(NB, n)
                weighted(NB, n)
            for tk in TAIL:
                task("tail", NB, tk)

        @block.scalar
        def _(act):
            def squares(i, n):
                r, t = n // T % RING, n % T
                if t == 0:
                    wait_side(act, "body", i, "pool", ("unit", n // T - 2) if n // T > 1 else None)
                act.wait_ge(s_max, i * STEPS + n + 1)
                act.wait_ge(s_sq, i * STEPS + n + 1)
                nc.scalar.activation(junk[:, n % 2, :], ps_s[:, n % 2, :], ACT.Exp, bias=negmax[:, r, t:t + 1],
                                     accum_out=sumsq[:, r, t:t + 1]).then_inc(s_sq, 1)

            def exp_t(i, n):
                act.wait_ge(s_pv, i * STEPS + n + 1)
                for c in range(2):
                    act.wait_ge(s_st, i * (2 * STEPS) + 2 * n + c + 1)
                    nc.scalar.activation(exps[:, n % RING, 512 * c:512 * c + 512], ps_t[:, c, :], ACT.Exp,
                                         scale=0.5).then_inc(s_exp, 1)

            def ident_act(dst, src, **kw):
                return nc.scalar.activation(dst, src, ACT.Identity, **kw)

            def copy(dst, src):
                return nc.scalar.activation(dst, src, ACT.Copy)

            def task(phase, i, tk):
                kind = tk[0]
                if "act" not in ENGINES[kind]:
                    return
                bank = bank_of(phase, tk)
                w = lambda of, t: wait_side(act, phase, i, of, t)
                if "pe" in ENGINES[kind]:
                    w("pe", tk)
                if kind == "snap":
                    w("pool", ("unit", 1))
                    last = nc.scalar.activation(gtmp[:, 0, :], dif_all[:, :, :].rearrange("p u t -> p (u t)"),
                                                ACT.Exp, scale=0.5)
                elif kind == "std":
                    w("pool", ("snap",))
                    for a in range(2):
                        last = nc.scalar.activation(
                            gin[:, :, :, 4 * a + 1].rearrange("p t h -> p h t"),
                            gtmp[:, 3, U * T // 2 * a:U * T // 2 * (a + 1)].rearrange("p (h t) -> p h t", h=H),
                            ACT.Sqrt)
                elif kind == "logit":
                    last = nc.scalar.activation(alpha_w[:, 0, :], bank[0:NW, 0:T * H], ACT.Tanh, bias=g3h[:, :],
                                                scale=0.5)
                elif kind == "attT":
                    last = copy(chan[:, 512 * tk[1]:512 * tk[1] + 512], bank[:, :])
                elif kind == "nT":
                    last = ident_act(chan[:, 512 * tk[1]:512 * tk[1] + 512], bank[:, :], scale=col[:, 2:3],
                                     bias=col[:, 3:4])
                elif kind == "attw":
                    last = ident_act(xa[:, CH * tk[1]:CH * tk[1] + CH], bank[:, 0:CH], bias=col[:, 1:2])
                elif kind == "fc1":
                    _, c, j = tk
                    if (c, j) == (0, 0):
                        act.wait_ge(s_exw, i * 64 + 64)
                    for q in range(2):
                        f = 2 * j + q
                        last = ident_act(hpre[:, f, CH * c:CH * c + CH], bank[:, CH * q:CH * q + CH],
                                         bias=fc1bs[:, f:f + 1])
                elif kind == "gelu1":
                    w("act", ("fc1", NC - 1, 1))
                    for f in range(FC):
                        last = nc.scalar.activation(hpre[:, f, :], hpre[:, f, :], ACT.Gelu)
                elif kind == "fc2":
                    last = ident_act(y[:, CH * tk[1]:CH * tk[1] + CH], bank[:, 0:CH], bias=fc2bs[:, :])
                elif kind == "gelu2":
                    w("dve", ("next", 1))
                    last = nc.scalar.activation(z[:, :, :], z[:, :, :], ACT.Gelu)
                elif kind == "embT":
                    last = copy(emb_t[:, 512 * tk[1]:512 * tk[1] + 512], bank[:, :])
                elif kind == "e2h":
                    if tk[1] == 0:
                        w("pool", None)
                    last = ident_act(xc[:, 0, 1 + 512 * tk[1]:513 + 512 * tk[1]], bank[:, :], bias=col[:, 0:1])
                elif kind in ("conva", "convg"):
                    _, l, c = tk
                    k = CONV.index(tk) // 2
                    if kind == "conva" and k >= 2:
                        w("pool", CONV[2 * (k - 2) + 1])
                    if kind == "conva":
                        last = ident_act(va[:, c % 2, :], bank[:, 0:CH], bias=cb[:, 2 * l:2 * l + 1])
                    else:
                        last = nc.scalar.activation(ug[:, c % 2, :], bank[:, CH:2 * CH], ACT.Tanh, scale=0.5,
                                                    bias=cb_half[:, 2 * l + 1:2 * l + 2])
                elif kind == "xnT":
                    last = copy(xn_t[:, 512 * tk[1]:512 * tk[1] + 512], bank[:, :])
                elif kind == "qk":
                    _, a, which, k = tk
                    at = QK[a].index(tk)
                    if at >= 2:
                        w("pool", QK[a][at - 2])
                    elif phase == "body":
                        w("pool", None)
                    last = ident_act(stage[:, k, :], bank[:, :], scale=0.5 if which == 0 else 1.0)
                last.then_inc(side_sem["act"], 1)

            act.wait_ge(s_init, 1)
            for dst, src in gate_loads:
                nc.scalar.dma_start(dst, src).then_inc(s_load, 16)
            act.wait_ge(s_load, 16 * N_LOADS)
            act.wait_ge(s_init, 3)
            nc.scalar.activation(g3h[:, :], g3b[:, :], ACT.Copy, scale=0.5)
            nc.scalar.activation(cb_half[:, :], cb[:, :], ACT.Copy, scale=0.5).then_inc(s_init, 1)
            act.wait_ge(s_init, 4)
            act.sem_inc(s_sq, 2)
            act.sem_inc(s_exp, 2)
            act.sem_inc(s_mrow, 64)
            for tk in PRE:
                task("pre", 0, tk)
            with act.Fori(0, NB // E) as group, act.Fori(0, E) as e:
                i = group * E + e
                for n in range(0, STEPS, 2):
                    exp_t(i, n)
                    squares(i, n)
                    for tk in STEP[n]:
                        task("body", i, tk)
                    squares(i, n + 1)
                    exp_t(i, n + 1)
                    for tk in STEP[n + 1]:
                        task("body", i, tk)
            for n in range(LAG_T):
                exp_t(NB, n)
            for tk in TAIL:
                task("tail", NB, tk)

        @block.vector
        def _(dve):
            pos = {"n": 0, "base": 0}

            def chain(i, ins):
                pos["n"] += 1
                ins.then_inc(s_dchain, 1)
                dve.wait_ge(s_dchain, i * pos["per"] + pos["base"] + pos["n"] if pos["loop"] else pos["base"] + pos["n"])

            def row_max(i, n):
                r, t = n // T % RING, n % T
                if t == 0:
                    wait_side(dve, "body", i, "pool", ("unit", n // T - 2) if n // T > 1 else None)
                dve.wait_ge(s_scores, i * STEPS + n + 1)
                nc.vector.tensor_reduce(negmax[:, r, t:t + 1], ps_s[:, n % 2, :], axis=AX, op=ALU.max, negate=True)\
                    .then_inc(s_max, 1)

            def row_min(i, n):
                r, t = n // T % RING, n % T
                dve.wait_ge(s_sq, i * STEPS + n + 3)
                nc.vector.tensor_reduce(rowmin[:, r, t:t + 1], ps_s[:, n % 2, :], axis=AX, op=ALU.min)\
                    .then_inc(s_min, 1)

            def divide(phase, i, j):
                u = (j - 2) % U
                if j == 2:
                    wait_side(dve, phase, i, "pool", ("snap",))
                dve.wait_ge(s_pv, i * STEPS + T * j + LAG_V % T + 2)
                nc.vector.transpose(o_t[:, :], ps_o[:, 0:QC]).then_inc(s_ot, 1)
                dve.wait_ge(s_ot, i * U + j + 1)
                o = o_t[:, :].rearrange("p (t c) -> p t c", t=T)
                chain(i, nc.vector.reciprocal(recip[:, u, :], o[:, :, HD]))
                nc.vector.tensor_tensor(mean_all[:, u, :], o[:, :, HD], recip[:, u, :], ALU.mult)
                return nc.vector.tensor_tensor(o_all[:, u, :, :], o[:, :, 0:HD],
                                               recip[:, u, :].unsqueeze(2).to_broadcast([P, T, HD]), ALU.mult)

            def moments(i, src, k):
                for t in range(T):
                    last = nc.vector.bn_stats(bn[:, t, :], src[:, t, :])
                chain(i, last)
                dve.nop(nofuse=True)
                for t in range(T):
                    last = nc.vector.bn_aggr(mv[:, k, t, :], bn[:, t, :])
                return last

            def task(phase, i, tk):
                kind = tk[0]
                if "dve" not in ENGINES[kind]:
                    return
                bank = bank_of(phase, tk)
                w = lambda of, t: wait_side(dve, phase, i, of, t)
                if "pe" in ENGINES[kind]:
                    w("pe", tk)
                four = bank[:, :].rearrange("p (q c) -> p q c", q=4)
                if kind == "mrow":
                    j = tk[1]
                    w("pool", ("msplit", j) if j else None)
                    dve.wait_ge(s_mrow, i * (U * 64) + 64 * (j + 1))
                    last = nc.vector.transpose(mrow[:, :], mparts[:, :, :].rearrange("p c t -> p (c t)"))
                elif kind == "unit":
                    wait_own(dve, phase, i, "dve", tk)
                    last = divide(phase, i, tk[1])
                elif kind == "win":
                    last = nc.vector.tensor_copy(winm[:, :], bank[0:H * 8, 0:T * NW])
                elif kind == "hid1":
                    last = nc.vector.tensor_scalar(hid1[:, :, :].rearrange("p g w -> p (g w)"), bank[:, :],
                                                   g1b[:, :], 0.0, ALU.add, ALU.max)
                elif kind == "hid2":
                    last = nc.vector.tensor_scalar(hid2[:, :, :].rearrange("p g w -> p (g w)"), bank[0:4 * HD, :],
                                                   g2b[:, :], 0.0, ALU.add, ALU.max)
                elif kind == "alpha":
                    last = nc.vector.tensor_copy(alpha_q[:, :], bank[:, 0:T * H])
                elif kind == "wo":
                    k = 4 * tk[1]
                    if k == 0:
                        w("pool", None)
                    last = nc.vector.tensor_tensor(h2[:, k:k + 4, :], four, h_cur[:, k:k + 4, :], ALU.add)
                elif kind == "ln2":
                    w("dve", ("wo", 1))
                    last = moments(i, h2, 0)
                elif kind == "ln3":
                    w("pool", ("ln2",))
                    last = moments(i, x2, 1)
                elif kind == "next":
                    k = 4 * tk[1]
                    if k == 0:
                        dve.wait_ge(s_out, i * 16 + 16)
                    last = nc.vector.tensor_tensor(z[:, k:k + 4, :], four,
                                                   row[:, 1, :].unsqueeze(1).to_broadcast([P, 4, P]), ALU.add)
                elif kind == "h2e":
                    k = 4 * tk[1]
                    if k == 0 and phase == "body":
                        w("pool", ("hcopy",))
                    last = nc.vector.tensor_tensor(h_next[:, k:k + 4, :], four,
                                                   row[:, 0, :].unsqueeze(1).to_broadcast([P, 4, P]), ALU.add)
                elif kind == "ln1":
                    w("dve", ("h2e", 1))
                    last = moments(i, h_next, 2)
                elif kind == "v":
                    k = 4 * tk[1]
                    if k == 0 and phase == "body":
                        w("pool", ("vcopy", 1))
                    for q in range(4):
                        last = nc.vector.tensor_copy(
                            v_next[:, k + q, :].rearrange("p (h c) -> p h c", h=H)[:, :, 0:HD],
                            four[:, q, :].rearrange("p (h c) -> p h c", h=H))
                last.then_inc(side_sem["dve"], 1)

            for t in (g1, g2, g3):
                last = nc.vector.memset(t[:].rearrange("p a b -> p (a b)") if len(t.shape) == 3 else t[:, :], 0.0)
            last.then_inc(s_init, 1)
            for t in (negmax, rowmin, sumsq):
                nc.vector.memset(t[:, :, :], 0.0)
            for t in (recip, mean_all, sq_all, dif_all):
                nc.vector.memset(t[:, :, :], 0.0)
            nc.vector.memset(exps[:, :, :], 1.0)
            nc.vector.memset(qst[:, :, :], 0.0)
            nc.vector.memset(kst[:, :, :], 0.0)
            nc.vector.memset(rs_pow[:, :], -0.5)
            nc.vector.memset(xc[:, :, 0:1], 0.0)
            last = nc.vector.memset(xc[:, :, L + 1:L + 2], 0.0)
            pos.update(loop=False, base=0, per=0)
            chain(0, last)
            last = nc.vector.memset(kst[KSC:KST, :, :], 1.0)
            last.then_inc(s_init, 1)
            dve.sem_inc(s_min, 2)
            dve.sem_inc(s_out, 16)
            dve.wait_ge(s_load, 16 * N_LOADS)
            dve.wait_ge(s_init, 4)
            for tk in PRE:
                task("pre", 0, tk)
            pos.update(loop=True, base=pos["n"], n=0, per=U + 3)
            with dve.Fori(0, NB // E) as group, dve.Fori(0, E) as e:
                i = group * E + e
                for n in range(0, STEPS, 2):
                    row_max(i, n)
                    row_max(i, n + 1)
                    for tk in STEP[n]:
                        task("body", i, tk)
                    row_min(i, n)
                    row_min(i, n + 1)
                    for tk in STEP[n + 1]:
                        task("body", i, tk)
            assert pos["n"] == pos["per"], pos
            pos.update(n=0)
            for tk in TAIL:
                task("tail", NB, tk)

        @block.gpsimd
        def _(pool):
            pos = {"n": 0, "base": 0, "loop": False, "per": 0}

            def chain(i, ins):
                pos["n"] += 1
                ins.then_inc(s_pchain, 1)
                pool.wait_ge(s_pchain, i * pos["per"] + pos["base"] + pos["n"] if pos["loop"]
                             else pos["base"] + pos["n"])

            tt = nc.gpsimd.tensor_tensor

            def ts(*args):
                pool.nop(nofuse=True)
                return nc.gpsimd.tensor_scalar(*args)

            def copy(dst, src):
                return ts(dst, src, 1.0, 1.0, ALU.mult, ALU.mult)

            def statistics(phase, i, j):
                u = (j - 2) % U
                r = u % RING
                wait_side(pool, phase, i, "dve", ("unit", j))
                pool.wait_ge(s_sq, i * STEPS + max(T * (j - 2) + T + 2, 2))
                if j == 2:
                    wait_side(pool, phase, i, "act", ("snap",))
                tt(dif_all[:, u, :], rowmin[:, r, :], negmax[:, r, :], ALU.add)
                chain(i, tt(sq_all[:, u, :], sumsq[:, r, :], recip[:, u, :], ALU.mult))
                return tt(sq_all[:, u, :], sq_all[:, u, :], recip[:, u, :], ALU.mult)

            def normalise(i, dst, src, k):
                chain(i, ts(rstd[:, k, :], mv[:, k, :, 1], 1.0, EPS, ALU.mult, ALU.add))
                chain(i, tt(rstd[:, k, :], rstd[:, k, :], rs_pow[:, :], ALU.pow))
                chain(i, tt(dst[:, :, :], src[:, :, :], mv[:, k, :, 0].unsqueeze(2).to_broadcast([P, T, P]),
                            ALU.subtract))
                return tt(dst[:, :, :], dst[:, :, :], rstd[:, k, :].unsqueeze(2).to_broadcast([P, T, P]), ALU.mult)

            def task(phase, i, tk):
                kind = tk[0]
                w = lambda of, t: wait_side(pool, phase, i, of, t)
                if kind == "gather":
                    b = 0 if phase == "pre" else i + 1
                    pool.wait_ge(s_idx, 16 if phase == "pre" else i * 16 + 32)
                    w("pe", None)
                    pool.nop(nofuse=True)
                    for t in range(T):
                        nc.gpsimd.indirect_dma_start(out=emb[:, t, :], out_offset=None, in_=table[:, :],
                                                     in_offset=bass.IndirectOffsetOnAxis(ap=idx[:, t:t + 1], axis=0))\
                            .then_inc(s_emb, 16)
                    return
                if "pool" not in ENGINES[kind]:
                    return
                wait_own(pool, phase, i, "pool", tk)
                if kind == "unit":
                    last = statistics(phase, i, tk[1])
                elif kind == "msplit":
                    j = tk[1]
                    r = (j - 1) % RING
                    pool.wait_ge(s_max, i * STEPS + T * j)
                    w("dve", ("mrow", j - 1))
                    chain(i, copy(mparts[:, 0, :], negmax[:, r, :]))
                    chain(i, tt(mrest[:, 0, :], negmax[:, r, :], mparts[:, 0, :], ALU.subtract))
                    chain(i, copy(mparts[:, 1, :], mrest[:, 0, :]))
                    last = tt(mparts[:, 2, :], mrest[:, 0, :], mparts[:, 1, :], ALU.subtract)
                elif kind == "vcopy":
                    if tk[1] == 0:
                        w("dve", None)
                        pool.wait_ge(s_pv, i * STEPS + 2)
                        last = copy(v_cur[:, :, 0:6 * VW], v_next[:, :, 0:6 * VW])
                    else:
                        pool.wait_ge(s_pv, i * STEPS + LAG_V - 1 + 3)
                        last = copy(v_cur[:, :, 6 * VW:H * VW], v_next[:, :, 6 * VW:])
                elif kind == "hcopy":
                    w("dve", ("wo", 1))
                    last = copy(h_cur[:, :, :], h_next[:, :, :])
                elif kind == "snap":
                    if phase == "body":
                        w("pe", None)
                    oa = o_all[:, :, :, :].rearrange("p u t d -> p t u d")
                    heads = lambda t: t[:, :, :].rearrange("p t (h d) -> p t h d", h=H)
                    tt(heads(odif), oa[:, :, 0:H, :], oa[:, :, H:U, :], ALU.subtract)
                    copy(heads(o2), oa[:, :, H:U, :])
                    flat = lambda t: t[:, :, :].rearrange("p u t -> p (u t)")

                    def feature(f, fn):
                        for a in range(2):
                            last = fn(gin[:, :, :, 4 * a + f].rearrange("p t h -> p h t"), a)
                        return last

                    def of(src, a):
                        return src[:, H * a:H * a + H, :]

                    def of2(k, a):
                        return gtmp[:, k, U * T // 2 * a:U * T // 2 * (a + 1)].rearrange("p (h t) -> p h t", h=H)
                    feature(0, lambda dst, a: ts(dst, of(mean_all, a), 1.0 / L, 1.0, ALU.mult, ALU.mult))
                    feature(2, lambda dst, a: copy(dst, of(recip, a)))
                    chain(i, tt(gtmp[:, 1, :], flat(mean_all), flat(mean_all), ALU.mult))
                    chain(i, ts(gtmp[:, 2, :], gtmp[:, 1, :], 1.0 / L, 1.0, ALU.mult, ALU.mult))
                    chain(i, tt(gtmp[:, 1, :], flat(sq_all), gtmp[:, 2, :], ALU.subtract))
                    chain(i, ts(gtmp[:, 3, :], gtmp[:, 1, :], 1.0 / (L - 1), 0.0, ALU.mult, ALU.max))
                    w("act", tk)
                    last = feature(3, lambda dst, a: tt(dst, of2(0, a), of(recip, a), ALU.mult))
                elif kind == "logit":
                    w("act", tk)
                    last = ts(alpha_w[:, 1, :], alpha_w[:, 0, :], 0.5, 0.5, ALU.mult, ALU.add)
                elif kind == "alpha":
                    w("dve", tk)
                    flat = lambda t: t[:, :, :].rearrange("p t (h d) -> p (t h) d", h=H)
                    chain(i, tt(flat(att), flat(odif), alpha_q[:, :].unsqueeze(2).to_broadcast([P, T * H, HD]),
                                ALU.mult))
                    last = tt(flat(att), flat(att), flat(o2), ALU.add)
                elif kind == "ln2":
                    w("dve", tk)
                    last = normalise(i, x2, h2, 0)
                elif kind == "ln3":
                    w("dve", tk)
                    w("pe", ("attT", 1))
                    last = normalise(i, att, x2, 1)
                elif kind == "gelu2":
                    w("act", tk)
                    last = tt(z[:, :, :], z[:, :, :], h2[:, :, :], ALU.add)
                elif kind == "convg":
                    _, l, c = tk
                    w("act", tk)
                    x_in = xc[:, l % 2, 1 + CH * c:1 + CH * c + CH]
                    x_out = xc[:, (l + 1) % 2, 1 + CH * c:1 + CH * c + CH]
                    chain(i, ts(ctmp[:, 0, :], ug[:, c % 2, :], 1.0, 0.5, ALU.add, ALU.mult))
                    chain(i, tt(ctmp[:, 1, :], ctmp[:, 0, :], va[:, c % 2, :], ALU.mult))
                    chain(i, tt(ctmp[:, 2, :], ctmp[:, 1, :], x_in, ALU.add))
                    last = ts(x_out, ctmp[:, 2, :], RES, 1.0, ALU.mult, ALU.mult)
                elif kind == "ln1":
                    w("dve", tk)
                    last = normalise(i, xn, h_next, 2)
                elif kind == "qk":
                    _, a, which, k = tk
                    w("act", tk)
                    dst = part[:, a, which, :, 512 * k:512 * k + 512]
                    chain(i, copy(dst[:, 0, :], stage[:, k, :]))
                    chain(i, tt(srest, stage[:, k, :], dst[:, 0, :], ALU.subtract))
                    chain(i, copy(dst[:, 1, :], srest))
                    last = tt(dst[:, 2, :], srest, dst[:, 1, :], ALU.subtract)
                last.then_inc(side_sem["pool"], 1)

            task("pre", 0, PRE[0])
            for t in (v_next, v_cur, h_cur):
                nc.gpsimd.memset(t[:, :, :], 0.0)
            nc.gpsimd.memset(mparts[:, :, :], 0.0)
            last = nc.gpsimd.memset(o_all[:, :, :, :], 0.0)
            chain(0, last)
            pool.wait_ge(s_load, 16 * N_LOADS)
            for t in (v_next, v_cur):
                last = nc.gpsimd.memset(t[:, :, 0:H * VW].rearrange("p t (h c) -> p t h c", c=VW)[:, :, :, HD:VW],
                                        1.0)
            last.then_inc(s_init, 1)
            pool.sem_inc(s_pv, 2)
            pool.wait_ge(s_init, 4)
            for tk in PRE[1:]:
                task("pre", 0, tk)
            per = 0
            for tk in BODY:
                per += {"msplit": 3, "unit": 1, "snap": 4, "alpha": 1, "ln2": 3, "ln3": 3, "convg": 3, "ln1": 3, "qk": 3}.get(tk[0], 0)
            pos.update(loop=True, base=pos["n"], n=0, per=per)
            with pool.Fori(0, NB // E) as group, pool.Fori(0, E) as e:
                i = group * E + e
                for n in range(STEPS):
                    for tk in STEP[n]:
                        task("body", i, tk)
            assert pos["n"] == pos["per"], pos
            pos.update(n=0)
            for tk in TAIL:
                task("tail", NB, tk)


def _constants():
    c = np.zeros((P, P + NW + P), np.float32)
    c[:, 0:P] = np.eye(P)
    for q in range(P):
        c[q, P + q // WS] = 1.0 / WS
        c[q // WS, P + NW + q] = 1.0
    return c


def kernel(**inputs):
    import concourse.bacc as _bacc
    from concourse.bass_utils import run_bass_kernel_spmd as _run

    a = {k: np.asarray(v) for k, v in inputs.items()}
    nb = a["x"].shape[0]
    ids = np.zeros((nb + 1, P, T), np.int32)
    ids[:nb] = a["x"].reshape(nb, T, P).transpose(0, 2, 1)
    f = {k[3:]: v for k, v in a.items() if k.startswith("L0_")}
    before = [(e - 1) % E for e in range(E)]
    arrays = {
        "ids": ids, "table": f["tok_emb_table"], "consts": _constants(),
        "w_e2h": f["tok_W_e2h"], "b_e2h": f["tok_b_e2h"].reshape(P, 1),
        "conv_w": f["tok_conv_w"].transpose(2, 0, 3, 1),
        "conv_b": f["tok_conv_b"].reshape(2 * LAYERS, P).T,
        "w_h2e": f["tok_W_h2e"], "b_h2e": f["tok_b_h2e"].reshape(1, P),
        "wq1": f["attn_Wq1"], "wk1": f["attn_Wk1"], "wq2": f["attn_Wq2"], "wk2": f["attn_Wk2"],
        "wv": f["attn_Wv"], "wo": f["attn_Wo"],
        "gw1": f["attn_gw1"], "gb1": f["attn_gb1"].reshape(-1, 1), "gw2": f["attn_gw2"],
        "gb2": f["attn_gb2"].reshape(-1, 1), "gw3": f["attn_gw3"], "gb3": f["attn_gb3"].reshape(1, 1),
        "ln_g": f["ffn_ln_g"].reshape(P, 1), "ln_b": f["ffn_ln_b"].reshape(P, 1),
        "attn_w": f["ffn_attn_w"].T, "attn_b": f["ffn_attn_b"].reshape(P, 1),
        "fc1_w": f["ffn_fc1_w"].transpose(0, 2, 1)[before],
        "fc1_b": f["ffn_fc1_b"].reshape(E, FC, P).transpose(0, 2, 1)[before],
        "fc2_w": f["ffn_fc2_w"].reshape(E, P, FC, P).transpose(0, 3, 2, 1)[before],
        "fc2_b": f["ffn_fc2_b"].reshape(E, P, 1)[before],
        "next_w": f["ffn_next_w"].T, "next_b": f["ffn_next_b"].reshape(1, P),
    }
    nc = _bacc.Bacc("TRN2", target_bir_lowering=False, num_devices=1)
    feed, args = {}, {}
    for name, v in arrays.items():
        v = np.ascontiguousarray(v)
        feed[f"in_{name}"] = v
        args[name] = nc.dram_tensor(f"in_{name}", v.shape, mybir.dt.from_np(v.dtype), kind="ExternalInput").ap()
    store = nc.dram_tensor("out_dram", (nb + 1, T, P, P), F32, kind="ExternalOutput").ap()
    tower_kernel(nc, out=store.rearrange("b t p d -> b p t d"), **args)
    r = _run(nc, [feed], core_ids=[0])
    return np.asarray(r.results[0]["out_dram"])[1:].reshape(nb, L, P)
```
